# Optimizing a Trainium2 kernel written in Bass

```python
import numpy as np
import jax
import jax.numpy as jnp

def _softmax(x, axis=-1):
    return jax.nn.softmax(x, axis=axis)

def _gelu(x):
    return jax.nn.gelu(x, approximate=True)

def _silu(x):
    return jax.nn.silu(x)

def _sigmoid(x):
    return jax.nn.sigmoid(x)

def _layernorm(x, axis=-1, eps=1e-05):
    m = jnp.mean(x, axis=axis, keepdims=True)
    v = jnp.var(x, axis=axis, keepdims=True)
    return (x - m) / jnp.sqrt(v + eps)

def _scatter_add(tgt, idx, src, axis=0):
    return tgt.at[idx].add(src)

def _segment_sum(src, seg, n):
    return jax.ops.segment_sum(src, seg, n)
kernel_name = 'mk_adaln_d1_jaxref_r8_6ee873'

def setup_inputs(seed: int=0):
    np.random.seed(seed)
    _w = jnp.asarray

    def _L0_attn_setup():
        import jax, jax.numpy as jnp
        import numpy as np
        B, T = (2, 256)
        DENSE = 128
        SPARSE = 128
        NH = 8
        HD = SPARSE // NH
        WINDOW = 64
        K = 32
        RANK = HD // 4
        GATE_THRESH = 0.2

        def _causal_window_indices(t_len, window):
            pos = jnp.arange(t_len)
            off = jnp.arange(window)
            idx = jnp.clip(pos[:, None] - off[None, :], 0, t_len - 1)
            mask = idx <= pos[:, None]
            return (idx, mask)

        def _dynamic_metric(field, w1, b1, w2, b2, base):
            sig = field.mean(axis=1)
            if field.shape[1] >= 8:
                sig = sig + field[:, ::8].mean(axis=1) * 0.5
            h = jax.nn.gelu(sig @ w1 + b1, approximate=False)
            mod = (h @ w2 + b2).reshape(field.shape[0], NH, HD)
            return jax.nn.softplus(base[None] + 0.1 * mod)
        key = jax.random.key(seed)
        ks = jax.random.split(key, 12)
        return {'x': jax.random.normal(ks[0], (B, T, DENSE), dtype=jnp.float32), 'enc_q': jax.random.normal(ks[1], (NH, DENSE, HD), dtype=jnp.float32) * 0.02, 'enc_v': jax.random.normal(ks[2], (NH, DENSE, HD), dtype=jnp.float32) * 0.02, 'metric_w1': jax.random.normal(ks[3], (SPARSE, SPARSE // 2), dtype=jnp.float32) * (1.0 / np.sqrt(SPARSE)), 'metric_b1': jnp.zeros((SPARSE // 2,), dtype=jnp.float32), 'metric_w2': jax.random.normal(ks[4], (SPARSE // 2, NH * HD), dtype=jnp.float32) * (1.0 / np.sqrt(SPARSE // 2)), 'metric_b2': jnp.zeros((NH * HD,), dtype=jnp.float32), 'base_metric': jnp.ones((NH, HD), dtype=jnp.float32) * 0.1, 'hebb_U': jax.random.normal(ks[5], (NH, HD, RANK), dtype=jnp.float32) * 0.01, 'hebb_V': jax.random.normal(ks[6], (NH, RANK, HD), dtype=jnp.float32) * 0.01, 'decoder': jax.random.normal(ks[7], (NH * HD, DENSE), dtype=jnp.float32) * 0.02}
    _L0_attn_in = _L0_attn_setup()

    def _L0_ffn_setup():
        import jax, jax.numpy as jnp
        import numpy as np
        B, N, D = (4, 256, 128)
        SPARSITY = 0.01
        key = jax.random.key(seed)
        k1, k2, k3 = jax.random.split(key, 3)
        x = jax.random.normal(k1, (B, N, D), dtype=jnp.float32)
        spatial = jax.random.normal(k2, (D, D), dtype=jnp.float32) * 0.02
        freq = jnp.fft.fft(spatial, axis=-1)
        k = int(D * SPARSITY)
        mag = jnp.abs(freq)
        kth = jax.lax.top_k(mag, k)[0][:, -1:]
        w_sparse = jnp.where(mag >= kth, freq, 0.0 + 0j)
        bias = jax.random.normal(k3, (D,), dtype=jnp.float32) * 0.01
        return {'x': x, 'w_freq_real': jnp.real(w_sparse).astype(jnp.float32), 'w_freq_imag': jnp.imag(w_sparse).astype(jnp.float32), 'bias': bias}
    _L0_ffn_in = _L0_ffn_setup()
    _L0_c = _w((lambda *s: np.random.randn(*s).astype(np.float32) * 0.05)(2, 128))
    _L0_wmod = _w((lambda *s: np.random.randn(*s).astype(np.float32) * 0.05)(128, 6 * 128) * 128 ** (-0.5))
    _d = {'L0_attn_x': _L0_attn_in['x'], 'L0_attn_enc_q': _L0_attn_in['enc_q'], 'L0_attn_enc_v': _L0_attn_in['enc_v'], 'L0_attn_metric_w1': _L0_attn_in['metric_w1'], 'L0_attn_metric_b1': _L0_attn_in['metric_b1'], 'L0_attn_metric_w2': _L0_attn_in['metric_w2'], 'L0_attn_metric_b2': _L0_attn_in['metric_b2'], 'L0_attn_base_metric': _L0_attn_in['base_metric'], 'L0_attn_hebb_U': _L0_attn_in['hebb_U'], 'L0_attn_hebb_V': _L0_attn_in['hebb_V'], 'L0_attn_decoder': _L0_attn_in['decoder'], 'L0_ffn_w_freq_real': _L0_ffn_in['w_freq_real'], 'L0_ffn_w_freq_imag': _L0_ffn_in['w_freq_imag'], 'L0_ffn_bias': _L0_ffn_in['bias'], 'L0_c': _L0_c, 'L0_wmod': _L0_wmod}
    _x0 = _d['L0_attn_x']
    _d['L0_attn_x'] = jax.random.normal(jax.random.fold_in(jax.random.key(seed), 1), (2, 2048, 128), dtype=_x0.dtype)
    del _x0
    return _d

def reference(L0_attn_x, L0_attn_enc_q, L0_attn_enc_v, L0_attn_metric_w1, L0_attn_metric_b1, L0_attn_metric_w2, L0_attn_metric_b2, L0_attn_base_metric, L0_attn_hebb_U, L0_attn_hebb_V, L0_attn_decoder, L0_ffn_w_freq_real, L0_ffn_w_freq_imag, L0_ffn_bias, L0_c, L0_wmod):

    def _L0_attn_ref(x, enc_q, enc_v, metric_w1, metric_b1, metric_w2, metric_b2, base_metric, hebb_U, hebb_V, decoder):
        import jax, jax.numpy as jnp
        import numpy as np
        B, T = (2, 256)
        DENSE = 128
        SPARSE = 128
        NH = 8
        HD = SPARSE // NH
        WINDOW = 64
        K = 32
        RANK = HD // 4
        GATE_THRESH = 0.2

        def _causal_window_indices(t_len, window):
            pos = jnp.arange(t_len)
            off = jnp.arange(window)
            idx = jnp.clip(pos[:, None] - off[None, :], 0, t_len - 1)
            mask = idx <= pos[:, None]
            return (idx, mask)

        def _dynamic_metric(field, w1, b1, w2, b2, base):
            sig = field.mean(axis=1)
            if field.shape[1] >= 8:
                sig = sig + field[:, ::8].mean(axis=1) * 0.5
            h = jax.nn.gelu(sig @ w1 + b1, approximate=False)
            mod = (h @ w2 + b2).reshape(field.shape[0], NH, HD)
            return jax.nn.softplus(base[None] + 0.1 * mod)
        Bb, Tt, _ = x.shape
        query_sparse = jax.nn.relu(jnp.einsum('btd,nde->btne', x, enc_q))
        value_sparse = jax.nn.relu(jnp.einsum('btd,nde->btne', x, enc_v))
        metric = _dynamic_metric(query_sparse.reshape(Bb, Tt, NH * HD), metric_w1, metric_b1, metric_w2, metric_b2, base_metric)
        idx, mask = _causal_window_indices(Tt, WINDOW)
        idx_b = jnp.broadcast_to(idx[None], (Bb, Tt, WINDOW))
        batch_ix = jnp.arange(Bb)[:, None, None]
        outs = []
        for h in range(NH):
            q_h = query_sparse[:, :, h, :]
            v_h = value_sparse[:, :, h, :]
            m_h = metric[:, h][:, None, None, :]
            k_windows = q_h[:, idx, :]
            diff = k_windows - q_h[:, :, None, :]
            dist = jnp.sqrt((diff * diff * m_h).sum(axis=-1) + 1e-08)
            dist = jnp.where(mask[None], dist, jnp.inf)
            neg_d, loc = jax.lax.top_k(-dist, K)
            topd = -neg_d
            top_idx = jnp.take_along_axis(idx_b, loc, axis=2)
            infl = jnp.exp(-topd)
            infl = infl / (infl.sum(axis=-1, keepdims=True) + 1e-08)
            neighbor_v = v_h[batch_ix, top_idx]
            context = jnp.einsum('btk,btkd->btd', infl, neighbor_v)
            q_norm = jnp.linalg.norm(q_h, axis=-1, keepdims=True)
            gate = (q_norm > GATE_THRESH).astype(q_h.dtype)
            heb_mat = hebb_U[h] @ hebb_V[h]
            q_unit = q_h / jnp.maximum(q_norm, 1e-12)
            heb_ctx = q_unit @ heb_mat
            context = context + gate * 0.1 * heb_ctx
            outs.append(q_h * context)
        out_sparse = jnp.stack(outs, axis=2)
        return out_sparse.reshape(Bb, Tt, NH * HD) @ decoder

    def _L0_ffn_ref(x, w_freq_real, w_freq_imag, bias):
        import jax, jax.numpy as jnp
        import numpy as np
        B, N, D = (4, 256, 128)
        SPARSITY = 0.01
        w = jax.lax.complex(w_freq_real, w_freq_imag)
        x_freq = jnp.fft.fft(x, axis=-1)
        y_freq = jnp.einsum('bnd,do->bno', x_freq, w)
        y = jnp.real(jnp.fft.ifft(y_freq, axis=-1))
        return y + bias
    x = L0_attn_x
    mod = (_silu(L0_c) @ L0_wmod).reshape(L0_c.shape[0], 6, 1, -1)
    sa, ca, ga, sb, cb, gb = (mod[:, 0], mod[:, 1], mod[:, 2], mod[:, 3], mod[:, 4], mod[:, 5])
    ga = (2 * (ga >= 0) - 1) * jnp.maximum(jnp.abs(ga), 0.25)
    gb = (2 * (gb >= 0) - 1) * jnp.maximum(jnp.abs(gb), 0.25)
    h = _layernorm(x, axis=-1) * (1 + ca) + sa
    x = x + ga * _L0_attn_ref(h, L0_attn_enc_q, L0_attn_enc_v, L0_attn_metric_w1, L0_attn_metric_b1, L0_attn_metric_w2, L0_attn_metric_b2, L0_attn_base_metric, L0_attn_hebb_U, L0_attn_hebb_V, L0_attn_decoder)
    h = _layernorm(x, axis=-1) * (1 + cb) + sb
    x = x + gb * _L0_ffn_ref(h, L0_ffn_w_freq_real, L0_ffn_w_freq_imag, L0_ffn_bias)
    return x

_drawn_inputs = setup_inputs


def setup_inputs(seed=0):
    import zlib

    import numpy as np

    out = dict(_drawn_inputs(seed))
    spreads = {'L0_attn_metric_b1': (0.0, 2.0),
     'L0_attn_metric_b2': (0.0, 2.0),
     'L0_attn_base_metric': (0.10000000149011612, 0.6)}
    factors = {'L0_attn_enc_q': 8.0,
     'L0_attn_enc_v': 8.0,
     'L0_attn_metric_w1': 8.0,
     'L0_attn_metric_w2': 8.0,
     'L0_attn_hebb_U': 64.0,
     'L0_attn_hebb_V': 64.0,
     'L0_attn_decoder': 8.0,
     'L0_ffn_bias': 27.577}
    for name, (base, spread) in spreads.items():
        noise = np.random.default_rng([zlib.crc32(name.encode()), seed]).standard_normal(out[name].shape)
        drawn = base * np.exp(spread * noise) if base else spread * noise
        out[name] = jnp.asarray(drawn.astype(out[name].dtype))
    for name, factor in factors.items():
        out[name] = (out[name] * factor).astype(out[name].dtype)
    return out
```

```python
import concourse.bass as bass
from concourse import mybir
from contextlib import ExitStack

F32 = mybir.dt.float32
BF16 = mybir.dt.bfloat16
ALU = mybir.AluOpType
ACT = mybir.ActivationFunctionType
AX = mybir.AxisListType.X

B, T, D = 2, 2048, 128
NH, HD, RANK = 8, 16, 4
WINDOW, TOPK = 64, 32
MLP = 64
P = 128
BLK = P // NH
SPAN = BLK - 1 + WINDOW
GB = 4
GQ = GB * BLK
PAIRS = B * T // P
PB = T // P
PAD = WINDOW
TP = T + PAD
UNIT = 512
UNITS = T // UNIT
UT = UNIT // P
ROUNDS = TOPK // 8
OUTSIDE = -2.0 ** 60
TAKEN = -2.0 ** 100
PQ = P // 4

CONST_COLS = {}
_at = 0
for _n, _w in (("ident", P), ("cos", P), ("sin", P), ("msin", P), ("cos_n", P), ("msin_n", P),
               ("head", NH), ("same_head", P), ("diag", BLK), ("window", SPAN), ("parity", 2 * PQ),
               ("row0", P), ("head_r", NH), ("minus_head", P)):
    CONST_COLS[_n] = (_at, _w)
    _at += _w
CONST_W = _at
WEIGHT_COLS = {}
_at = 0
for _n, _w in (("c_t", B), ("wmod", 6 * D), ("enc_q", D), ("enc_v", D), ("w1", MLP), ("w2", D), ("b1", 1),
               ("b2", 1), ("base", 1), ("u_t", HD), ("v", HD), ("decoder", D), ("w_re", D),
               ("w_im", D), ("bias", D)):
    WEIGHT_COLS[_n] = (_at, _w)
    _at += _w
WEIGHT_W = _at


def build(nc, x, weights, consts, out):
    ctx = ExitStack()
    with ctx:
        def sb(name, shape, dt=F32):
            return ctx.enter_context(nc.sbuf_tensor(name, shape, dt))

        def sem(name):
            return ctx.enter_context(nc.semaphore(name))

        X = sb("X", [P, PAIRS, D])
        CO = sb("CO", [P, CONST_W])
        WE = sb("WE", [P, WEIGHT_W])

        def co(name):
            a, w = CONST_COLS[name]
            return CO[:, a:a + w]

        def we(name):
            a, w = WEIGHT_COLS[name]
            return WE[:, a:a + w]

        ident = co("ident")
        HT = sb("HT", [P, B * TP])
        Q = sb("Q", [P, B * TP])
        Q2 = sb("Q2", [P, B * TP])
        ident_b = sb("ident_b", [P, P], BF16)
        window_b = sb("window_b", [P, SPAN], BF16)
        XN1 = sb("XN1", [P, 2, UNIT])
        stats1 = sb("stats1", [P, PAIRS, 6])
        mv1 = sb("mv1", [P, PAIRS, 2])
        lnv1 = sb("lnv1", [P, PAIRS])
        rstd1 = sb("rstd1", [P, PAIRS])
        silu_c = sb("silu_c", [P, 4, B])
        silu_rows = sb("silu_rows", [P, B, P])
        mod = sb("mod", [P, 6, B])
        gates = sb("gates", [P, 2, B, D])
        gate_abs = sb("gate_abs", [P, 2, B, D])
        gate_sign = sb("gate_sign", [P, 2, B, D])
        DEC = sb("DEC", [P, B, D])
        R1T = sb("R1T", [P, D])
        R2T = sb("R2T", [P, D])
        FF = sb("FF", [P, B, D])
        FB = sb("FB", [P, B, D])
        UB = sb("UB", [NH * RANK, NH, HD])
        HEB = sb("HEB", [P, NH, HD])
        qsum = sb("qsum", [P, B, UNITS])
        esum = sb("esum", [P, B, UNITS])
        sig = sb("sig", [P, 3, B])
        mlp = sb("mlp", [MLP, B])
        met = sb("met", [P, 6, B])
        bb = sb("bb", [P, 2])
        eps = sb("eps", [P, 4])
        HM2 = sb("HM2", [P, B, NH])
        QM2 = sb("QM2", [P, B * TP])
        HV = sb("HV", [P, 2, P])
        A = sb("A", [P, 2, GB, NH, BLK])
        S = sb("S", [P, 2, GB, SPAN])
        R = sb("R", [P, 2, GB, SPAN])
        DG = sb("DG", [P, 2, GB, BLK])
        SELF = sb("SELF", [P, 2, GB])
        Y = sb("Y", [P, 2, GB, SPAN])
        top8 = sb("top8", [P, GB, 8])
        W = sb("W", [P, 2, GB, P])
        WT = sb("WT", [P, 2, GB, NH, BLK])
        V = sb("V", [P, 2, 2, P])
        DEN = sb("DEN", [P, P])
        RD = sb("RD", [P, P])
        CN = sb("CN", [P, P])
        LQ = sb("LQ", [P, P])
        IQ = sb("IQ", [P, P])
        QH = sb("QH", [P, P])
        G0 = sb("G0", [P, P])
        G = sb("G", [P, P])
        CG = sb("CG", [P, P])
        O = sb("O", [P, P])
        X1 = sb("X1", [P, D])
        stats2 = sb("stats2", [P, 6])
        mv2 = sb("mv2", [P, 2])
        lnv2 = sb("lnv2", [P, 1])
        rstd2 = sb("rstd2", [P, 1])
        XN2 = sb("XN2", [P, D])
        H2 = sb("H2", [P, P])
        OUT = sb("OUT", [P, D])

        bank = [ctx.enter_context(nc.psum_tensor(f"bank{k}", [P, 512], F32)) for k in range(8)]
        pS = [bank[k][:, 0:GB * SPAN].rearrange("p (k j) -> p k j", k=GB) for k in range(2)]
        pW = [bank[2 + k][:, :].rearrange("p (k c) -> p k c", k=GB) for k in range(2)]
        pV = bank[4][:, 0:P]
        pC = bank[5][:, 0:P]
        pD = bank[5][:, P:2 * P]
        pN = bank[6][:, 0:P]
        pH = bank[6][:, P:2 * P]
        pA = bank[7][:, 0:P]
        pT = bank[7][:, P:2 * P]
        pY = bank[7][:, 2 * P:3 * P]

        x_loaded = [sem(f"x_loaded{b}") for b in range(B)]
        weights_loaded = sem("weights_loaded")
        consts_loaded = sem("consts_loaded")
        cleared = sem("cleared")
        pool_step = sem("pool_step")
        pe_step = sem("pe_step")
        act_step = sem("act_step")
        dve_step = sem("dve_step")
        xn1_ready = sem("xn1_ready")
        xt1_ready = sem("xt1_ready")
        h_ready = sem("h_ready")
        qmm_ready = sem("qmm_ready")
        q_ready = sem("q_ready")
        q2_ready = sem("q2_ready")
        e_summed = sem("e_summed")
        mod_ready = sem("mod_ready")
        stats1_ready = sem("stats1_ready")
        rstd1_ready = sem("rstd1_ready")
        setup_done = sem("setup_done")
        expanded = sem("expanded")
        scores_ready = sem("scores_ready")
        scores_copied = sem("scores_copied")
        self_ready = sem("self_ready")
        dist2_ready = sem("dist2_ready")
        chain = sem("chain")
        expdist_ready = sem("expdist_ready")
        weights_ready = sem("weights_ready")
        wt_ready = sem("wt_ready")
        wt_copied = sem("wt_copied")
        frame_copied = sem("frame_copied")
        v_ready = sem("v_ready")
        v_copied = sem("v_copied")
        context_ready = sem("context_ready")
        diag_masked = sem("diag_masked")
        top8_found = sem("top8_found")
        marked = sem("marked")
        stats2_found = sem("stats2_found")
        den_ready = sem("den_ready")
        rden_ready = sem("rden_ready")
        cn_ready = sem("cn_ready")
        norms_ready = sem("norms_ready")
        lnq_ready = sem("lnq_ready")
        invq_ready = sem("invq_ready")
        qh_copied = sem("qh_copied")
        gate_ready = sem("gate_ready")
        heb_ready = sem("heb_ready")
        cg_ready = sem("cg_ready")
        o_ready = sem("o_ready")
        att_ready = sem("att_ready")
        x1_ready = sem("x1_ready")
        mv2_ready = sem("mv2_ready")
        lnv2_ready = sem("lnv2_ready")
        rstd2_ready = sem("rstd2_ready")
        xn2_ready = sem("xn2_ready")
        xt2_ready = sem("xt2_ready")
        h2_ready = sem("h2_ready")
        y_ready = sem("y_ready")
        out_ready = sem("out_ready")
        stored = sem("stored")

        LAG = 3

        def need(eng, s, value):
            if not isinstance(value, int) or value > 0:
                eng.wait_ge(s, value)

        def known(k, count):
            return not isinstance(k, int) or 0 <= k < count

        def column(i, u=0):
            return i * P + (i // PB) * PAD + u * GQ

        def run(eng, body):
            for i in range(LAG):
                body(i)
            with eng.Fori(LAG, PAIRS) as i:
                body(i)
            for i in range(PAIRS, PAIRS + LAG):
                body(i)

        block = ctx.enter_context(nc.Block())

        @block.sync
        def _(sp):
            half = x.shape[0] // 2
            sp.dma_start(X[:, 0:PB, :], x[0, :, :].rearrange("(k p) d -> p k d", p=P)).then_inc(x_loaded[0], 16)
            sp.dma_start(X[:, PB:2 * PB, :], x[1, :, :].rearrange("(k p) d -> p k d", p=P)).then_inc(x_loaded[1], 16)

            def store(i):
                k = i - 2
                if known(k, PAIRS):
                    need(sp, out_ready, k + 1)
                    sp.dma_start(out[bass.ds(k * P, P), :], OUT[:, :]).then_inc(stored, 16)

            run(sp, store)
            sp.wait_ge(stored, 16 * PAIRS)

        @block.gpsimd
        def _(pool):
            g = nc.gpsimd
            g.memset(W[:], 0.0).then_inc(cleared, 1)
            g.memset(V[:], 0.0).then_inc(cleared, 1)
            for b in range(B):
                base = b * TP
                with pool.Fori(0, UNITS) as w:
                    cols = bass.ds(base + w * UNIT, UNIT)
                    pool.wait_ge(q_ready, b * UNITS + w + 1)
                    g.tensor_tensor(Q2[:, cols], Q[:, cols], Q[:, cols], ALU.mult).then_inc(q2_ready, 1)
                pool.wait_ge(q2_ready, (b + 1) * UNITS)
                for arr in (HT, Q, Q2):
                    last = base + T
                    g.tensor_copy(arr[:, last:last + PAD],
                                  arr[:, last - 1:last].to_broadcast([P, PAD])).then_inc(pool_step, 1)
            pool.wait_ge(setup_done, 1)
            pool.wait_ge(pool_step, 3 * B)

            def expand(i, u):
                n = 2 * i + u
                if known(n, 2 * PAIRS):
                    need(pool, scores_ready, n - 1)
                    q = Q[:, bass.ds(column(i, u), GQ)].rearrange("p (k h t) -> p k h t", k=GB, h=1)
                    m = HM2[:, (i // PB), :].rearrange("p (k h t) -> p k h t", k=1, t=1)
                    g.tensor_tensor(A[:, u], q.to_broadcast([P, GB, NH, BLK]),
                                    m.to_broadcast([P, GB, NH, BLK]), ALU.mult).then_inc(expanded, 1)

            def frame(i, u):
                n = 2 * i + u
                if known(n, 2 * PAIRS):
                    need(pool, v_ready, n - 1)
                    g.tensor_copy(HV[:, u], HT[:, bass.ds(column(i, u), P)]).then_inc(frame_copied, 1)

            def distance(n, u):
                if known(n, 2 * PAIRS):
                    need(pool, self_ready, n + 1)
                    g.tensor_tensor(Y[:, u], SELF[:, u, :].rearrange("p (k o) -> p k o", o=1).to_broadcast([P, GB, SPAN]),
                                    S[:, u], ALU.subtract).then_inc(dist2_ready, 1)

            def gated(k):
                if known(k, PAIRS):
                    need(pool, heb_ready, k + 1)
                    need(pool, cn_ready, k + 1)
                    g.tensor_tensor(CG[:], CN[:], G[:], ALU.add).then_inc(cg_ready, 1)
                    need(pool, cg_ready, k + 1)
                    g.tensor_tensor(O[:], CG[:], Q[:, bass.ds(column(k), P)], ALU.mult).then_inc(o_ready, 1)

            def hebbian(k):
                if known(k, PAIRS):
                    need(pool, gate_ready, k + 1)
                    need(pool, qh_copied, k + 1)
                    need(pool, o_ready, k)
                    g.tensor_tensor(G[:], G0[:], QH[:], ALU.mult).then_inc(heb_ready, 1)

            def body(i):
                distance(2 * i - 1, 1)
                expand(i, 0)
                gated(i - 2)
                distance(2 * i, 0)
                expand(i, 1)
                hebbian(i - 1)
                frame(i, 0)
                frame(i, 1)

            run(pool, body)

        @block.scalar
        def _(act):
            a = nc.scalar
            act.dma_start(WE[:], weights[:, :]).then_inc(weights_loaded, 16)
            act.dma_start(CO[:], consts[:, :]).then_inc(consts_loaded, 16)
            steps = [0]

            def done(ins):
                steps[0] += 1
                ins.then_inc(act_step, 1)
                return steps[0]

            act.wait_ge(weights_loaded, 16)
            act.wait_ge(dve_step, 1)
            done(a.activation(silu_c[:, 0], we("c_t"), ACT.Exp, scale=-1.0))
            for b in range(B):
                tiles = slice(b * PB, (b + 1) * PB)
                act.wait_ge(stats1_ready, b + 1)
                k = done(a.activation(lnv1[:, tiles], mv1[:, tiles, 1], ACT.Ln, bias=eps[:, 0:1]))
                act.wait_ge(act_step, k)
                a.activation(rstd1[:, tiles], lnv1[:, tiles], ACT.Exp, scale=-0.5).then_inc(rstd1_ready, 1)
            act.wait_ge(mod_ready, 1)
            for b in range(B):
                with act.Fori(0, UNITS) as w:
                    cols = bass.ds(b * TP + w * UNIT, UNIT)
                    act.wait_ge(xt1_ready, b * UNITS + w + 1)
                    a.activation(HT[:, cols], bank[0][:, :], ACT.Identity,
                                 bias=mod[:, 0, b:b + 1], scale=mod[:, 1, b:b + 1]).then_inc(h_ready, 1)
                    act.wait_ge(qmm_ready, b * UNITS + w + 1)
                    a.activation(Q[:, cols], bank[1][:, :], ACT.Relu,
                                 accum_out=qsum[:, b, bass.ds(w, 1)]).then_inc(q_ready, 1)
            act.wait_ge(pe_step, 2)
            done(a.activation(gate_abs[:], bank[3][:, :], ACT.Abs))
            act.wait_ge(pe_step, 7)
            done(a.activation(mlp[:], bank[2][0:MLP, 0:B], ACT.Gelu, bias=we("b1")[0:MLP, :]))
            act.wait_ge(pe_step, 8)
            act.wait_ge(dve_step, 4)
            k = done(a.activation(met[:, 0], bank[2][:, 0:B], ACT.Identity, bias=bb[:, 1:2], scale=0.1))
            act.wait_ge(act_step, k)
            k = done(a.activation(met[:, 1], met[:, 0], ACT.Abs))
            act.wait_ge(act_step, k)
            k = done(a.activation(met[:, 2], met[:, 1], ACT.Exp, scale=-1.0))
            act.wait_ge(act_step, k)
            done(a.activation(met[:, 3], met[:, 2], ACT.Ln, bias=1.0))
            act.wait_ge(setup_done, 1)

            def scores(n, u):
                if known(n, 2 * PAIRS):
                    need(act, scores_ready, n + 1)
                    need(act, weights_ready, n - 1)
                    a.activation(S[:, u], pS[u], ACT.Copy).then_inc(scores_copied, 1)

            def exp_distance(n, u):
                if known(n, 2 * PAIRS):
                    need(act, dist2_ready, n + 1)
                    a.activation(Y[:, u], Y[:, u], ACT.Relu).then_inc(chain, 1)
                    need(act, chain, 3 * n + 1)
                    a.activation(Y[:, u], Y[:, u], ACT.Ln, bias=eps[:, 1:2]).then_inc(chain, 1)
                    need(act, chain, 3 * n + 2)
                    a.activation(Y[:, u], Y[:, u], ACT.Exp, scale=0.5).then_inc(chain, 1)
                    need(act, chain, 3 * n + 3)
                    a.activation(Y[:, u], Y[:, u], ACT.Exp, scale=-1.0).then_inc(expdist_ready, 1)

            def values(n, u):
                if known(n, 2 * PAIRS):
                    need(act, v_ready, n + 1)
                    need(act, context_ready, n - 1)
                    dst = V[:, u].rearrange("p s (a s2 d) -> p a s s2 d", s2=2, d=HD)
                    for s in range(2):
                        ins = a.activation(dst[:, :, s, s, :],
                                           pV.rearrange("p (a s d) -> p a s d", s=2, d=HD)[:, :, s, :], ACT.Relu)
                    ins.then_inc(v_copied, 1)

            def weights_t(n, u):
                if known(n, 2 * PAIRS):
                    need(act, wt_ready, n + 1)
                    need(act, context_ready, n - 1)
                    a.activation(WT[:, u], pW[u], ACT.Copy).then_inc(wt_copied, 1)

            def denominator(k):
                if known(k, PAIRS):
                    need(act, context_ready, 2 * k + 2)
                    a.activation(DEN[:], pD, ACT.Identity, bias=eps[:, 1:2]).then_inc(den_ready, 1)

            def query_norm(k):
                if known(k, PAIRS):
                    need(act, norms_ready, k + 1)
                    a.activation(LQ[:], pN, ACT.Ln, bias=eps[:, 2:3]).then_inc(lnq_ready, 1)
                    a.activation(QH[:], pH, ACT.Copy, scale=0.1).then_inc(qh_copied, 1)
                    need(act, lnq_ready, k + 1)
                    a.activation(IQ[:], LQ[:], ACT.Exp, scale=-0.5).then_inc(invq_ready, 1)

            def rstd(k):
                if known(k, PAIRS):
                    need(act, mv2_ready, k + 1)
                    a.activation(lnv2[:], mv2[:, 1:2], ACT.Ln, bias=eps[:, 0:1]).then_inc(lnv2_ready, 1)
                    need(act, lnv2_ready, k + 1)
                    a.activation(rstd2[:], lnv2[:], ACT.Exp, scale=-0.5).then_inc(rstd2_ready, 1)

            def modulate(k):
                if known(k, PAIRS):
                    need(act, xt2_ready, k + 1)
                    b = k // PB
                    a.activation(H2[:], pT, ACT.Identity, bias=mod[:, 3, bass.ds(b, 1)],
                                 scale=mod[:, 4, bass.ds(b, 1)]).then_inc(h2_ready, 1)

            def body(i):
                denominator(i - 2)
                exp_distance(2 * i - 1, 1)
                modulate(i - 3)
                scores(2 * i, 0)
                values(2 * i - 2, 0)
                weights_t(2 * i - 2, 0)
                exp_distance(2 * i, 0)
                rstd(i - 2)
                scores(2 * i + 1, 1)
                query_norm(i - 1)
                values(2 * i - 1, 1)
                weights_t(2 * i - 1, 1)

            run(act, body)

        @block.vector
        def _(dve):
            v = nc.vector
            steps = [0]

            def done(ins):
                steps[0] += 1
                ins.then_inc(dve_step, 1)
                return steps[0]

            def then(ins):
                dve.wait_ge(dve_step, done(ins))

            for c, e in enumerate((1e-5, 1e-8, 1e-18)):
                last = v.memset(eps[:, c:c + 1], e)
            done(last)
            dve.wait_ge(act_step, 1)
            then(v.tensor_scalar(silu_c[:, 1], silu_c[:, 0], 1.0, None, ALU.add))
            then(v.reciprocal(silu_c[:, 2], silu_c[:, 1]))
            then(v.scalar_tensor_tensor(bb[:, 1:2], we("b2"), 0.1, we("base"), ALU.mult, ALU.add))
            then(v.tensor_tensor(silu_c[:, 3], silu_c[:, 2], we("c_t"), ALU.mult))
            for b in range(B):
                last = v.tensor_copy(silu_rows[:, b], silu_c[:, 3, b:b + 1].to_broadcast([P, P]))
            done(last)
            for b in range(B):
                dve.wait_ge(x_loaded[b], 16)
                for k in range(b * PB, (b + 1) * PB):
                    last = v.bn_stats(stats1[:, k], X[:, k])
                then(last)
                for k in range(b * PB, (b + 1) * PB):
                    last = v.bn_aggr(mv1[:, k], stats1[:, k])
                last.then_inc(stats1_ready, 1)
            dve.wait_ge(pe_step, 1)
            pm = bank[2][:, 0:6 * B].rearrange("p (j b) -> p j b", b=B)
            for j, add in ((0, 0.0), (1, 1.0), (3, 0.0), (4, 1.0)):
                last = v.tensor_scalar(mod[:, j], pm[:, j], add, None, ALU.add)
            last.then_inc(mod_ready, 1)
            dve.wait_ge(consts_loaded, 16)
            v.tensor_copy(ident_b[:], ident)
            done(v.tensor_copy(window_b[:], co("window")))
            for b in range(B):
                dve.wait_ge(rstd1_ready, b + 1)
                with dve.Fori(0, UNITS) as w:
                    dve.wait_ge(xt1_ready, b * UNITS + w) if b else None
                    for c in range(UT):
                        k = b * PB + w * UT + c
                        ins = v.tensor_scalar(XN1[:, 0, c * P:(c + 1) * P], X[:, bass.ds(k, 1), :],
                                              mv1[:, bass.ds(k, 1), 0], rstd1[:, bass.ds(k, 1)],
                                              ALU.subtract, ALU.mult)
                    ins.then_inc(xn1_ready, 1)
                    dve.wait_ge(q_ready, b * UNITS + w + 1)
                    v.tensor_reduce(esum[:, b, bass.ds(w, 1)],
                                    Q[:, bass.ds(b * TP + w * UNIT, UNIT)].rearrange("p (n e) -> p n e", e=8)[:, :, 7],
                                    AX, ALU.add).then_inc(e_summed, 1)
            dve.wait_ge(e_summed, B * UNITS)
            v.tensor_reduce(sig[:, 0], qsum[:], AX, ALU.add)
            then(v.tensor_reduce(sig[:, 1], esum[:], AX, ALU.add))
            then(v.tensor_scalar(sig[:, 0], sig[:, 0], 1.0 / T, None, ALU.mult))
            done(v.scalar_tensor_tensor(sig[:, 2], sig[:, 1], 0.5 / (T // 8), sig[:, 0], ALU.mult, ALU.add))
            dve.wait_ge(act_step, 4)
            v.tensor_scalar(gate_sign[:], bank[3][:, :].rearrange("p (j b d) -> p j b d", j=2, b=B), 0.0, 2.0,
                            ALU.is_ge, ALU.mult)
            then(v.tensor_scalar(gate_abs[:], gate_abs[:], 0.25, None, ALU.max))
            then(v.scalar_tensor_tensor(gates[:], gate_sign[:], -1.0, gate_abs[:], ALU.add, ALU.mult))
            r32 = NH * RANK
            done(v.tensor_tensor(
                UB[:], we("u_t")[0:r32, :].rearrange("p (h d) -> p h d", h=1).to_broadcast([r32, NH, HD]),
                co("head_r")[0:r32, :].rearrange("p (h d) -> p h d", d=1).to_broadcast([r32, NH, HD]), ALU.mult))
            dve.wait_ge(pe_step, 3)
            v.tensor_copy(R1T[:], bank[4][:, 0:D])
            done(v.tensor_copy(R2T[:], bank[4][:, D:2 * D]))
            dve.wait_ge(pe_step, 6)
            for b in range(B):
                v.tensor_tensor(DEC[:, b], we("decoder"), gates[:, 0, b], ALU.mult)
                v.tensor_tensor(FF[:, b], bank[5][:, 0:D], gates[:, 1, b], ALU.mult)
                v.tensor_tensor(FB[:, b], we("bias"), gates[:, 1, b], ALU.mult)
            v.tensor_tensor(HEB[:], bank[6][:, 0:HD].rearrange("p (h d) -> p h d", h=1).to_broadcast([P, NH, HD]),
                            co("head").rearrange("p (h d) -> p h d", d=1).to_broadcast([P, NH, HD]), ALU.mult)
            dve.wait_ge(act_step, 9)
            then(v.scalar_tensor_tensor(met[:, 4], met[:, 0], 0.0, met[:, 3], ALU.max, ALU.add))
            dve.wait_ge(pool_step, 3 * B)
            for b in range(B):
                v.tensor_scalar(HM2[:, b], co("head"), met[:, 4, b:b + 1], 2.0, ALU.mult, ALU.mult)
                last = v.tensor_scalar(QM2[:, b * TP:(b + 1) * TP], Q2[:, b * TP:(b + 1) * TP],
                                       met[:, 4, b:b + 1], None, ALU.mult)
            last.then_inc(setup_done, 1)
            dve.wait_ge(setup_done, 1)
            dve.wait_ge(cleared, 2)

            def own_scores(n, u):
                need(dve, scores_copied, n + 1)
                v.tensor_tensor(DG[:, u], S[:, u, :, 0:BLK],
                                co("diag").rearrange("p (k t) -> p k t", k=1).to_broadcast([P, GB, BLK]),
                                ALU.mult).then_inc(diag_masked, 1)
                dve.wait_ge(diag_masked, 1)
                v.tensor_reduce(SELF[:, u], DG[:, u], AX, ALU.add).then_inc(self_ready, 1)

            def take8(r, u):
                src = R if r else S
                for k in range(GB):
                    if r:
                        dve.wait_ge(marked, GB * (r - 1) + k + 1)
                    v.max(top8[:, k], src[:, u, k]).then_inc(top8_found, 1)
                for k in range(GB):
                    dve.wait_ge(top8_found, GB * r + k + 1)
                    v.match_replace(R[:, u, k], top8[:, k], src[:, u, k], TAKEN).then_inc(marked, 1)

            def end_group():
                dve.wait_ge(marked, GB * ROUNDS)
                dve.sem_clear(marked)
                dve.sem_clear(top8_found)
                dve.sem_clear(diag_masked)
                dve.sem_clear(stats2_found)

            def weigh(n, u):
                if known(n, 2 * PAIRS):
                    need(dve, expdist_ready, n + 1)
                    need(dve, wt_ready, n - 1)
                    frame = bass.AP(tensor=W[:, u].tensor, offset=W[:, u].offset,
                                    ap=[list(W[:, u].ap[0]), [P + BLK, GB], [1, SPAN]])
                    v.scalar_tensor_tensor(frame, R[:, u], TAKEN, Y[:, u], ALU.is_equal,
                                           ALU.mult).then_inc(weights_ready, 1)

            def normalise(k):
                if known(k, PAIRS):
                    need(dve, den_ready, k + 1)
                    v.reciprocal(RD[:], DEN[:]).then_inc(rden_ready, 1)
                    need(dve, rden_ready, k + 1)
                    v.tensor_tensor(CN[:], pC, RD[:], ALU.mult).then_inc(cn_ready, 1)

            def gate(k):
                if known(k, PAIRS):
                    need(dve, invq_ready, k + 1)
                    v.scalar_tensor_tensor(G0[:], pN, 0.04, IQ[:], ALU.is_gt, ALU.mult).then_inc(gate_ready, 1)

            def residual(k):
                if known(k, PAIRS):
                    need(dve, att_ready, k + 1)
                    v.tensor_tensor(X1[:], pA, X[:, bass.ds(k, 1), :], ALU.add).then_inc(x1_ready, 1)
                    need(dve, x1_ready, k + 1)
                    v.bn_stats(stats2[:], X1[:]).then_inc(stats2_found, 1)
                    dve.wait_ge(stats2_found, 1)
                    v.bn_aggr(mv2[:], stats2[:]).then_inc(mv2_ready, 1)

            def normed(k):
                if known(k, PAIRS):
                    need(dve, rstd2_ready, k + 1)
                    v.tensor_scalar(XN2[:], X1[:], mv2[:, 0:1], rstd2[:], ALU.subtract,
                                    ALU.mult).then_inc(xn2_ready, 1)

            def result(k):
                if known(k, PAIRS):
                    need(dve, y_ready, k + 1)
                    need(dve, stored, 16 * k)
                    v.tensor_tensor(OUT[:], pY, X1[:], ALU.add).then_inc(out_ready, 1)

            def body(i):
                more = known(i, PAIRS)
                for u in range(2):
                    if more:
                        own_scores(2 * i + u, u)
                        take8(0, u)
                    if u == 0:
                        residual(i - 2)
                    else:
                        gate(i - 1)
                        normed(i - 2)
                    if more:
                        take8(1, u)
                    weigh(2 * i + u - 1, 1 - u)
                    if u == 1:
                        normalise(i - 1)
                    if more:
                        take8(2, u)
                    if u == 1:
                        result(i - 2)
                    if more:
                        take8(3, u)
                        end_group()
                    else:
                        dve.drain()
                        dve.sem_clear(stats2_found)

            run(dve, body)

        @block.tensor
        def _(pe):
            t = nc.tensor
            pe.wait_ge(weights_loaded, 16)
            pe.wait_ge(dve_step, 6)
            for j in range(6):
                last = t.matmul(bank[2][:, j * B:(j + 1) * B], we("wmod")[:, j * D:(j + 1) * D], silu_c[:, 3],
                                start=True, stop=True)
            last.then_inc(pe_step, 1)
            for n, j in enumerate((2, 5)):
                for b in range(B):
                    at = (n * B + b) * D
                    last = t.matmul(bank[3][:, at:at + D], silu_rows[:, b], we("wmod")[:, j * D:(j + 1) * D],
                                    start=True, stop=True)
            last.then_inc(pe_step, 1)
            pe.wait_ge(consts_loaded, 16)
            for n, (w0, m0, w1, m1) in enumerate((("w_re", "cos", "w_im", "sin"), ("w_im", "cos", "w_re", "msin"))):
                o = bank[4][:, n * D:(n + 1) * D]
                t.matmul(o, we(w0), co(m0), start=True, stop=False)
                last = t.matmul(o, we(w1), co(m1), start=False, stop=True)
            last.then_inc(pe_step, 1)
            for b in range(B):
                with pe.Fori(0, UNITS) as w:
                    pe.wait_ge(xn1_ready, b * UNITS + w + 1)
                    if b:
                        pe.wait_ge(h_ready, b * UNITS + w)
                    for c in range(UT):
                        last = t.transpose(bank[0][:, c * P:(c + 1) * P], XN1[:, 0, c * P:(c + 1) * P], ident)
                    last.then_inc(xt1_ready, 1)
                    pe.wait_ge(h_ready, b * UNITS + w + 1)
                    t.matmul(bank[1][:, :], we("enc_q"), HT[:, bass.ds(b * TP + w * UNIT, UNIT)],
                             start=True, stop=True).then_inc(qmm_ready, 1)
            pe.wait_ge(dve_step, 15)
            r32 = NH * RANK
            t.matmul(bank[6][:, 0:HD], UB[:].rearrange("p h d -> p (h d)"), we("v")[0:r32, :],
                     start=True, stop=True).then_inc(pe_step, 1)
            pe.wait_ge(dve_step, 16)
            t.matmul(bank[5][:, 0:D], R1T[:], co("cos_n"), start=True, stop=False).then_inc(pe_step, 1)
            t.matmul(bank[5][:, 0:D], R2T[:], co("msin_n"), start=False, stop=True).then_inc(pe_step, 1)
            t.matmul(bank[2][0:MLP, 0:B], we("w1"), sig[:, 2], start=True, stop=True).then_inc(pe_step, 1)
            pe.wait_ge(act_step, 5)
            t.matmul(bank[2][:, 0:B], we("w2")[0:MLP, :], mlp[:], start=True, stop=True).then_inc(pe_step, 1)
            pe.wait_ge(setup_done, 1)
            pe.wait_ge(pool_step, 3 * B)

            def scores(i, u):
                n = 2 * i + u
                if known(n, 2 * PAIRS):
                    need(pe, expanded, n + 1)
                    need(pe, scores_copied, n - 1)
                    for k in range(GB):
                        keys = bass.ds(column(i, u) + k * BLK, SPAN)
                        t.matmul(pS[u][:, k], A[:, u, k].rearrange("p h t -> p (h t)"), Q[:, keys],
                                 start=True, stop=False)
                        t.matmul(pS[u][:, k], co("minus_head"), QM2[:, keys],
                                 start=False, stop=False)
                        last = t.matmul(pS[u][:, k], ident_b[:], window_b[:], start=False, stop=True)
                    last.then_inc(scores_ready, 1)

            def values(i, u):
                n = 2 * i + u
                if known(n, 2 * PAIRS):
                    need(pe, v_copied, n)
                    need(pe, frame_copied, n + 1)
                    t.matmul(pV, HV[:, u], we("enc_v"), start=True,
                             stop=True).then_inc(v_ready, 1)

            def weights_t(n, u):
                if known(n, 2 * PAIRS):
                    need(pe, weights_ready, n + 1)
                    need(pe, wt_copied, n - 1)
                    for k in range(GB):
                        last = t.transpose(pW[u][:, k], W[:, u, k], ident)
                    last.then_inc(wt_ready, 1)

            def context(i, u):
                n = 2 * i + u
                if known(n, 2 * PAIRS):
                    need(pe, wt_copied, n + 1)
                    need(pe, v_copied, n + 1)
                    need(pe, cn_ready, i)
                    ones = co("parity").rearrange("p (s c) -> p s c", s=2)
                    for dst, src in ((pC, None), (pD, ones)):
                        for a in range(4):
                            for s in range(2):
                                lhs = V[:, u, s, a * PQ:(a + 1) * PQ] if src is None else src[:, s, :]
                                last = t.matmul(dst[a * PQ:(a + 1) * PQ, u * GQ:(u + 1) * GQ], lhs,
                                                WT[:, u, :, 2 * a + s, :], start=(s == 0), stop=(s == 1))
                    last.then_inc(context_ready, 1)

            def norms(k):
                if known(k, PAIRS):
                    need(pe, heb_ready, k)
                    cols = bass.ds(column(k), P)
                    t.matmul(pN, co("same_head"), Q2[:, cols], start=True, stop=True)
                    t.matmul(pH, HEB[:].rearrange("p h d -> p (h d)"), Q[:, cols], start=True,
                             stop=True).then_inc(norms_ready, 1)

            def attention(k):
                if known(k, PAIRS):
                    need(pe, o_ready, k + 1)
                    need(pe, out_ready, k)
                    t.matmul(pA, O[:], DEC[:, bass.ds(k // PB, 1)].rearrange("p o d -> p (o d)"), start=True,
                             stop=True).then_inc(att_ready, 1)

            def normed_t(k):
                if known(k, PAIRS):
                    need(pe, xn2_ready, k + 1)
                    t.transpose(pT, XN2[:], ident).then_inc(xt2_ready, 1)

            def feed_forward(k):
                if known(k, PAIRS):
                    need(pe, h2_ready, k + 1)
                    b = bass.ds(k // PB, 1)
                    t.matmul(pY, H2[:], FF[:, b].rearrange("p o d -> p (o d)"), start=True, stop=False)
                    t.matmul(pY, co("row0"), FB[:, b].rearrange("p o d -> p (o d)"), start=False,
                             stop=True).then_inc(y_ready, 1)

            def body(i):
                scores(i, 0)
                values(i - 1, 0)
                normed_t(i - 3)
                weights_t(2 * i - 2, 0)
                feed_forward(i - 3)
                context(i - 1, 0)
                norms(i - 1)
                scores(i, 1)
                values(i - 1, 1)
                attention(i - 2)
                weights_t(2 * i - 1, 1)
                context(i - 1, 1)

            run(pe, body)


def _constants():
    import numpy as np
    c = np.zeros((P, CONST_W), np.float32)

    def put(name, value):
        a, w = CONST_COLS[name]
        value = np.asarray(value)
        c[:value.shape[0], a:a + w] = value

    p = np.arange(P)
    angle = 2 * np.pi * ((p[:, None] * p[None, :]) % D) / D
    put("ident", np.eye(P))
    put("cos", np.cos(angle))
    put("sin", np.sin(angle))
    put("msin", -np.sin(angle))
    put("cos_n", np.cos(angle) / D)
    put("msin_n", -np.sin(angle) / D)
    put("head", p[:, None] // HD == np.arange(NH)[None, :])
    put("same_head", p[:, None] // HD == p[None, :] // HD)
    q = p % BLK
    put("diag", q[:, None] == np.arange(BLK)[None, :])
    off = np.arange(SPAN)[None, :] - q[:, None]
    put("window", np.where((off >= 0) & (off < WINDOW), 0.0, OUTSIDE))
    put("parity", np.broadcast_to(np.arange(2 * PQ)[None, :] // PQ == (np.arange(2 * PQ)[None, :] % PQ) // HD, (P, 2 * PQ)))
    put("row0", np.broadcast_to(p[:, None] == 0, (P, P)))
    put("minus_head", -1.0 * (p[:, None] // HD == p[None, :] // BLK))
    put("head_r", np.arange(NH * RANK)[:, None] // RANK == np.arange(NH)[None, :])
    return c


def kernel(**inputs):
    import numpy as np
    import concourse.bacc as bacc
    from concourse.bass_utils import run_bass_kernel_spmd

    given = {k[3:]: np.asarray(a) for k, a in inputs.items()}
    w = np.zeros((P, WEIGHT_W), np.float32)
    for name, a in (
        ("c_t", given["c"].T), ("wmod", given["wmod"]),
        ("enc_q", given["attn_enc_q"].transpose(1, 0, 2).reshape(D, D)),
        ("enc_v", given["attn_enc_v"].transpose(1, 0, 2).reshape(D, D)),
        ("w1", given["attn_metric_w1"]), ("w2", given["attn_metric_w2"]),
        ("b1", given["attn_metric_b1"].reshape(-1, 1)), ("b2", given["attn_metric_b2"].reshape(-1, 1)),
        ("base", given["attn_base_metric"].reshape(-1, 1)),
        ("u_t", given["attn_hebb_U"].transpose(0, 2, 1).reshape(NH * RANK, HD)),
        ("v", given["attn_hebb_V"].reshape(NH * RANK, HD)),
        ("decoder", given["attn_decoder"]), ("w_re", given["ffn_w_freq_real"]),
        ("w_im", given["ffn_w_freq_imag"]), ("bias", given["ffn_bias"].reshape(1, D)),
    ):
        at, width = WEIGHT_COLS[name]
        w[:a.shape[0], at:at + width] = a
    arrays = {"x": np.ascontiguousarray(given["attn_x"][:, ::-1, :]), "weights": w, "consts": _constants()}

    nc = bacc.Bacc("TRN2", target_bir_lowering=False, num_devices=1)
    aps = [nc.dram_tensor(n, a.shape, F32, kind="ExternalInput").ap() for n, a in arrays.items()]
    aps.append(nc.dram_tensor("out", (B * T, D), F32, kind="ExternalOutput").ap())
    build(nc, *aps)
    r = run_bass_kernel_spmd(nc, [arrays], core_ids=[0])
    return np.ascontiguousarray(r.results[0]["out"].reshape(B, T, D)[:, ::-1, :])
```

```python
import concourse.bass as bass
from concourse import mybir
from contextlib import ExitStack

F32 = mybir.dt.float32
BF16 = mybir.dt.bfloat16
ALU = mybir.AluOpType
ACT = mybir.ActivationFunctionType
AX = mybir.AxisListType.X

B, T, D = 2, 2048, 128
NH, HD, RANK = 8, 16, 4
WINDOW, TOPK = 64, 32
MLP = 64
P = 128
BLK = P // NH
SPAN = BLK - 1 + WINDOW
GB = 4
GQ = GB * BLK
PAIRS = B * T // P
PB = T // P
PAD = WINDOW
TP = T + PAD
UNIT = 512
UNITS = T // UNIT
UT = UNIT // P
ROUNDS = TOPK // 8
OUTSIDE = -2.0 ** 60
LEFT_OUT = 1024.0
TAKEN = -2.0 ** 100
PQ = P // 4

CONST_COLS = {}
_at = 0
for _n, _w in (("ident", P), ("cos", P), ("sin", P), ("msin", P), ("cos_n", P), ("msin_n", P),
               ("head", NH), ("same_head", P), ("diag", BLK), ("window", SPAN), ("parity", 2 * PQ),
               ("row0", P), ("head_r", NH), ("minus_head", P)):
    CONST_COLS[_n] = (_at, _w)
    _at += _w
CONST_W = _at
WEIGHT_COLS = {}
_at = 0
for _n, _w in (("c_t", B), ("wmod", 6 * D), ("enc_q", D), ("enc_v", D), ("w1", MLP), ("w2", D), ("b1", 1),
               ("b2", 1), ("base", 1), ("u_t", HD), ("v", HD), ("decoder", D), ("w_re", D),
               ("w_im", D), ("bias", D)):
    WEIGHT_COLS[_n] = (_at, _w)
    _at += _w
WEIGHT_W = _at


def build(nc, x, weights, consts, out):
    ctx = ExitStack()
    with ctx:
        def sb(name, shape, dt=F32):
            return ctx.enter_context(nc.sbuf_tensor(name, shape, dt))

        def sem(name):
            return ctx.enter_context(nc.semaphore(name))

        X = sb("X", [P, PAIRS, D])
        CO = sb("CO", [P, CONST_W])
        WE = sb("WE", [P, WEIGHT_W])

        def co(name):
            a, w = CONST_COLS[name]
            return CO[:, a:a + w]

        def we(name):
            a, w = WEIGHT_COLS[name]
            return WE[:, a:a + w]

        ident = co("ident")
        HT = sb("HT", [P, B * TP])
        Q = sb("Q", [P, B * TP])
        Q2 = sb("Q2", [P, B * TP])
        ident_b = sb("ident_b", [P, P], BF16)
        window_b = sb("window_b", [P, SPAN], BF16)
        XN1 = sb("XN1", [P, 2, UNIT])
        stats1 = sb("stats1", [P, PAIRS, 6])
        mv1 = sb("mv1", [P, PAIRS, 2])
        lnv1 = sb("lnv1", [P, PAIRS])
        rstd1 = sb("rstd1", [P, PAIRS])
        silu_c = sb("silu_c", [P, 4, B])
        silu_rows = sb("silu_rows", [P, B, P])
        mod = sb("mod", [P, 6, B])
        gates = sb("gates", [P, 2, B, D])
        gate_abs = sb("gate_abs", [P, 2, B, D])
        gate_sign = sb("gate_sign", [P, 2, B, D])
        DEC = sb("DEC", [P, B, D])
        R1T = sb("R1T", [P, D])
        R2T = sb("R2T", [P, D])
        FF = sb("FF", [P, B, D])
        FB = sb("FB", [P, B, D])
        UB = sb("UB", [NH * RANK, NH, HD])
        HEB = sb("HEB", [P, NH, HD])
        qsum = sb("qsum", [P, B, UNITS])
        esum = sb("esum", [P, B])
        sig = sb("sig", [P, 3, B])
        mlp = sb("mlp", [MLP, B])
        met = sb("met", [P, 6, B])
        bb = sb("bb", [P, 2])
        eps = sb("eps", [P, 4])
        HM2 = sb("HM2", [P, B, NH])
        QM2 = sb("QM2", [P, B * TP])
        HV = sb("HV", [P, 2, P])
        A = sb("A", [P, 2, GB, NH, BLK])
        S = sb("S", [P, 2, GB, SPAN])
        R = sb("R", [P, 2, GB, SPAN])
        DG = sb("DG", [P, 2, GB, BLK])
        SELF = sb("SELF", [P, 2, GB])
        Y = sb("Y", [P, 2, GB, SPAN])
        U = sb("U", [P, 2, GB, SPAN])
        top8 = sb("top8", [P, GB, 8])
        W = sb("W", [P, 2, GB, P])
        WT = sb("WT", [P, 2, GB, NH, BLK])
        V = sb("V", [P, 2, 2, P])
        DEN = sb("DEN", [P, P])
        LD = sb("LD", [P, P])
        RD = sb("RD", [P, P])
        CN = sb("CN", [P, P])
        ND = sb("ND", [P, 2, P])
        two = sb("two", [P, 1])
        CR = sb("CR", [P, P])
        LQ = sb("LQ", [P, P])
        IQ = sb("IQ", [P, P])
        QH = sb("QH", [P, P])
        G0 = sb("G0", [P, P])
        G = sb("G", [P, P])
        CG = sb("CG", [P, P])
        O = sb("O", [P, P])
        X1 = sb("X1", [P, D])
        stats2 = sb("stats2", [P, 6])
        mv2 = sb("mv2", [P, 2])
        lnv2 = sb("lnv2", [P, 1])
        rstd2 = sb("rstd2", [P, 1])
        XN2 = sb("XN2", [P, D])
        H2 = sb("H2", [P, P])
        OUT = sb("OUT", [P, D])

        bank = [ctx.enter_context(nc.psum_tensor(f"bank{k}", [P, 512], F32)) for k in range(8)]
        pS = [bank[k][:, 0:GB * SPAN].rearrange("p (k j) -> p k j", k=GB) for k in range(2)]
        pW = [bank[2 + k][:, :].rearrange("p (k c) -> p k c", k=GB) for k in range(2)]
        pV = bank[4][:, 0:P]
        pC = bank[5][:, 0:P]
        pD = bank[5][:, P:2 * P]
        pN = bank[6][:, 0:P]
        pH = bank[6][:, P:2 * P]
        pA = bank[7][:, 0:P]
        pT = bank[7][:, P:2 * P]
        pY = bank[7][:, 2 * P:3 * P]

        x_loaded = [sem(f"x_loaded{b}") for b in range(B)]
        weights_loaded = sem("weights_loaded")
        consts_loaded = sem("consts_loaded")
        cleared = sem("cleared")
        pool_step = sem("pool_step")
        pe_step = sem("pe_step")
        act_step = sem("act_step")
        dve_step = sem("dve_step")
        xn1_ready = sem("xn1_ready")
        xt1_ready = sem("xt1_ready")
        h_ready = sem("h_ready")
        qmm_ready = sem("qmm_ready")
        q_ready = sem("q_ready")
        q2_ready = sem("q2_ready")
        e_summed = sem("e_summed")
        mod_ready = sem("mod_ready")
        stats1_ready = sem("stats1_ready")
        rstd1_ready = sem("rstd1_ready")
        setup_done = sem("setup_done")
        expanded = sem("expanded")
        scores_ready = sem("scores_ready")
        scores_copied = sem("scores_copied")
        self_ready = sem("self_ready")
        dist2_ready = sem("dist2_ready")
        chain = sem("chain")
        distance_ready = sem("distance_ready")
        group_taken = sem("group_taken")
        left_out_ready = sem("left_out_ready")
        exponent_ready = sem("exponent_ready")
        weights_ready = sem("weights_ready")
        wt_ready = sem("wt_ready")
        wt_copied = sem("wt_copied")
        frame_copied = sem("frame_copied")
        v_ready = sem("v_ready")
        v_copied = sem("v_copied")
        context_ready = sem("context_ready")
        diag_masked = [sem(f"diag_masked{u}") for u in range(2)]
        top8_found = sem("top8_found")
        marked = sem("marked")
        stats2_found = sem("stats2_found")
        den_ready = sem("den_ready")
        lnden_ready = sem("lnden_ready")
        rden_ready = sem("rden_ready")
        cn_ready = sem("cn_ready")
        norms_ready = sem("norms_ready")
        lnq_ready = sem("lnq_ready")
        invq_ready = sem("invq_ready")
        qh_copied = sem("qh_copied")
        gate_ready = sem("gate_ready")
        heb_ready = sem("heb_ready")
        newton_step = sem("newton_step")
        o_ready = sem("o_ready")
        att_ready = sem("att_ready")
        x1_ready = sem("x1_ready")
        mv2_ready = sem("mv2_ready")
        lnv2_ready = sem("lnv2_ready")
        rstd2_ready = sem("rstd2_ready")
        xn2_ready = sem("xn2_ready")
        xt2_ready = sem("xt2_ready")
        h2_ready = sem("h2_ready")
        y_ready = sem("y_ready")
        out_ready = sem("out_ready")
        stored = sem("stored")

        LAG = 3

        def need(eng, s, value):
            if not isinstance(value, int) or value > 0:
                eng.wait_ge(s, value)

        def known(k, count):
            return not isinstance(k, int) or 0 <= k < count

        def column(i, u=0):
            return i * P + (i // PB) * PAD + u * GQ

        def run(eng, body):
            for i in range(LAG):
                body(i)
            with eng.Fori(LAG, PAIRS) as i:
                body(i)
            for i in range(PAIRS, PAIRS + LAG):
                body(i)

        def unit_cols(w):
            at = (w // UNITS) * TP + (w % UNITS) * UNIT
            return slice(at, at + UNIT)

        block = ctx.enter_context(nc.Block())

        @block.sync
        def _(sp):
            half = x.shape[0] // 2
            sp.dma_start(X[:, 0:PB, :], x[0, :, :].rearrange("(k p) d -> p k d", p=P)).then_inc(x_loaded[0], 16)
            sp.dma_start(X[:, PB:2 * PB, :], x[1, :, :].rearrange("(k p) d -> p k d", p=P)).then_inc(x_loaded[1], 16)

            def store(i):
                k = i - 2
                if known(k, PAIRS):
                    need(sp, out_ready, k + 1)
                    sp.dma_start(out[bass.ds(k * P, P), :], OUT[:, :]).then_inc(stored, 16)

            run(sp, store)
            sp.wait_ge(stored, 16 * PAIRS)

        @block.gpsimd
        def _(pool):
            g = nc.gpsimd
            g.memset(W[:], 0.0).then_inc(cleared, 1)
            g.memset(V[:], 0.0).then_inc(cleared, 1)
            g.memset(two[:], 2.0).then_inc(cleared, 1)
            for b in range(B):
                base = b * TP
                for w in range(UNITS):
                    cols = bass.ds(base + w * UNIT, UNIT)
                    pool.wait_ge(q_ready, b * UNITS + w + 1)
                    g.tensor_tensor(Q2[:, cols], Q[:, cols], Q[:, cols], ALU.mult).then_inc(q2_ready, 1)
                pool.wait_ge(q2_ready, (b + 1) * UNITS)
                for arr in (HT, Q, Q2):
                    last = base + T
                    g.tensor_copy(arr[:, last:last + PAD],
                                  arr[:, last - 1:last].to_broadcast([P, PAD])).then_inc(pool_step, 1)
            pool.wait_ge(setup_done, 1)
            pool.wait_ge(pool_step, 3 * B)

            def expand(i, u):
                n = 2 * i + u
                if known(n, 2 * PAIRS):
                    need(pool, scores_ready, n - 1)
                    q = Q[:, bass.ds(column(i, u), GQ)].rearrange("p (k h t) -> p k h t", k=GB, h=1)
                    m = HM2[:, (i // PB), :].rearrange("p (k h t) -> p k h t", k=1, t=1)
                    g.tensor_tensor(A[:, u], q.to_broadcast([P, GB, NH, BLK]),
                                    m.to_broadcast([P, GB, NH, BLK]), ALU.mult).then_inc(expanded, 1)

            def frame(i, u):
                n = 2 * i + u
                if known(n, 2 * PAIRS):
                    need(pool, v_ready, n - 1)
                    g.tensor_copy(HV[:, u], HT[:, bass.ds(column(i, u), P)]).then_inc(frame_copied, 1)

            def distance(n, u):
                if known(n, 2 * PAIRS):
                    need(pool, self_ready, n + 1)
                    g.tensor_tensor(Y[:, u], SELF[:, u, :].rearrange("p (k o) -> p k o", o=1).to_broadcast([P, GB, SPAN]),
                                    S[:, u], ALU.subtract).then_inc(dist2_ready, 1)

            def exponent(n, u):
                if known(n, 2 * PAIRS):
                    need(pool, left_out_ready, n + 1)
                    g.tensor_tensor(Y[:, u], Y[:, u], U[:, u], ALU.add).then_inc(exponent_ready, 1)

            def gated(k):
                if known(k, PAIRS):
                    need(pool, heb_ready, k + 1)
                    need(pool, cn_ready, k + 1)
                    g.tensor_tensor(ND[:, 0], DEN[:], RD[:], ALU.mult).then_inc(newton_step, 1)
                    need(pool, newton_step, 4 * k + 1)
                    g.tensor_tensor(ND[:, 1], two[:, 0:1].to_broadcast([P, P]), ND[:, 0],
                                    ALU.subtract).then_inc(newton_step, 1)
                    need(pool, newton_step, 4 * k + 2)
                    g.tensor_tensor(CR[:], CN[:], ND[:, 1], ALU.mult).then_inc(newton_step, 1)
                    need(pool, newton_step, 4 * k + 3)
                    g.tensor_tensor(CG[:], CR[:], G[:], ALU.add).then_inc(newton_step, 1)
                    need(pool, newton_step, 4 * k + 4)
                    g.tensor_tensor(O[:], CG[:], Q[:, bass.ds(column(k), P)], ALU.mult).then_inc(o_ready, 1)

            def hebbian(k):
                if known(k, PAIRS):
                    need(pool, gate_ready, k + 1)
                    need(pool, qh_copied, k + 1)
                    need(pool, o_ready, k)
                    g.tensor_tensor(G[:], G0[:], QH[:], ALU.mult).then_inc(heb_ready, 1)

            def body(i):
                distance(2 * i - 2, 0)
                exponent(2 * i - 3, 1)
                expand(i, 0)
                frame(i - 1, 0)
                frame(i - 1, 1)
                distance(2 * i - 1, 1)
                exponent(2 * i - 2, 0)
                expand(i, 1)
                hebbian(i - 2)
                gated(i - 2)

            run(pool, body)

        @block.scalar
        def _(act):
            a = nc.scalar
            act.dma_start(WE[:], weights[:, :]).then_inc(weights_loaded, 16)
            act.dma_start(CO[:], consts[:, :]).then_inc(consts_loaded, 16)
            steps = [0]

            def done(ins):
                steps[0] += 1
                ins.then_inc(act_step, 1)
                return steps[0]

            TABLE = "natural_log_exp_and_others"
            a.preload_act_table_set(TABLE)
            act.wait_ge(weights_loaded, 16)
            act.wait_ge(dve_step, 1)
            done(a.activation(silu_c[:, 0], we("c_t"), ACT.Exp, scale=-1.0))
            def rstd_all(b):
                tiles = slice(b * PB, (b + 1) * PB)
                act.wait_ge(stats1_ready, b + 1)
                k = done(a.activation(lnv1[:, tiles], mv1[:, tiles, 1], ACT.Ln, bias=eps[:, 0:1]))
                act.wait_ge(act_step, k)
                a.activation(rstd1[:, tiles], lnv1[:, tiles], ACT.Exp, scale=-0.5).then_inc(rstd1_ready, 1)

            def modulated(w):
                b = w // UNITS
                act.wait_ge(xt1_ready, w + 1)
                a.activation(HT[:, unit_cols(w)], bank[w % 2][:, :], ACT.Identity,
                             bias=mod[:, 0, b:b + 1], scale=mod[:, 1, b:b + 1]).then_inc(h_ready, 1)

            def queries(w):
                act.wait_ge(qmm_ready, w + 1)
                a.activation(Q[:, unit_cols(w)], bank[6 + w % 2][:, :], ACT.Relu,
                             accum_out=qsum[:, w // UNITS, w % UNITS:w % UNITS + 1]).then_inc(q_ready, 1)

            rstd_all(0)
            act.wait_ge(mod_ready, 1)
            modulated(0)
            for w in range(B * UNITS):
                if w == 1:
                    rstd_all(1)
                if w + 1 < B * UNITS:
                    modulated(w + 1)
                queries(w)
            act.wait_ge(pe_step, 2)
            done(a.activation(gate_abs[:], bank[3][:, :], ACT.Abs))
            act.wait_ge(pe_step, 7)
            done(a.activation(mlp[:], bank[2][0:MLP, 0:B], ACT.Gelu, bias=we("b1")[0:MLP, :]))
            a.preload_act_table_set(TABLE)
            act.wait_ge(pe_step, 8)
            act.wait_ge(dve_step, 4)
            k = done(a.activation(met[:, 0], bank[2][:, 0:B], ACT.Identity, bias=bb[:, 1:2], scale=0.1))
            act.wait_ge(act_step, k)
            k = done(a.activation(met[:, 1], met[:, 0], ACT.Abs))
            act.wait_ge(act_step, k)
            k = done(a.activation(met[:, 2], met[:, 1], ACT.Exp, scale=-1.0))
            act.wait_ge(act_step, k)
            done(a.activation(met[:, 3], met[:, 2], ACT.Ln, bias=1.0))
            act.wait_ge(setup_done, 1)

            def scores(n, u):
                if known(n, 2 * PAIRS):
                    need(act, scores_ready, n + 1)
                    a.activation(S[:, u], pS[u], ACT.Copy).then_inc(scores_copied, 1)

            def distance(n, u):
                if known(n, 2 * PAIRS):
                    need(act, dist2_ready, n + 1)
                    a.activation(Y[:, u], Y[:, u], ACT.Relu).then_inc(chain, 1)
                    need(act, chain, 2 * n + 1)
                    a.activation(Y[:, u], Y[:, u], ACT.Ln, bias=eps[:, 1:2]).then_inc(chain, 1)
                    need(act, chain, 2 * n + 2)
                    a.activation(Y[:, u], Y[:, u], ACT.Exp, scale=0.5).then_inc(distance_ready, 1)

            def left_out(n, u):
                if known(n, 2 * PAIRS):
                    need(act, group_taken, n + 1)
                    a.activation(U[:, u], R[:, u], ACT.Relu, bias=eps[:, 3:4],
                                 scale=LEFT_OUT / -OUTSIDE).then_inc(left_out_ready, 1)

            def weigh(n, u):
                if known(n, 2 * PAIRS):
                    need(act, exponent_ready, n + 1)
                    need(act, wt_ready, n - 1)
                    w = W[:, u]
                    frame = bass.AP(tensor=w.tensor, offset=w.offset,
                                    ap=[list(w.ap[0]), [P + BLK, GB], [1, SPAN]])
                    a.activation(frame, Y[:, u], ACT.Exp, scale=-1.0).then_inc(weights_ready, 1)

            def values(n, u):
                if known(n, 2 * PAIRS):
                    need(act, v_ready, n + 1)
                    need(act, context_ready, n - 1)
                    dst = V[:, u].rearrange("p s (a s2 d) -> p a s s2 d", s2=2, d=HD)
                    for s in range(2):
                        ins = a.activation(dst[:, :, s, s, :],
                                           pV.rearrange("p (a s d) -> p a s d", s=2, d=HD)[:, :, s, :], ACT.Relu)
                    ins.then_inc(v_copied, 1)

            def weights_t(n, u):
                if known(n, 2 * PAIRS):
                    need(act, wt_ready, n + 1)
                    need(act, context_ready, n - 1)
                    a.activation(WT[:, u], pW[u], ACT.Copy).then_inc(wt_copied, 1)

            def denominator(k):
                if known(k, PAIRS):
                    need(act, context_ready, 2 * k + 2)
                    a.activation(LD[:], pD, ACT.Ln, bias=eps[:, 1:2]).then_inc(lnden_ready, 1)
                    a.activation(DEN[:], pD, ACT.Identity, bias=eps[:, 1:2]).then_inc(den_ready, 1)
                    need(act, lnden_ready, k + 1)
                    a.activation(RD[:], LD[:], ACT.Exp, scale=-1.0).then_inc(rden_ready, 1)

            def query_norm(k):
                if known(k, PAIRS):
                    need(act, norms_ready, k + 1)
                    a.activation(LQ[:], pN, ACT.Ln, bias=eps[:, 2:3]).then_inc(lnq_ready, 1)
                    a.activation(QH[:], pH, ACT.Copy, scale=0.1).then_inc(qh_copied, 1)
                    need(act, lnq_ready, k + 1)
                    a.activation(IQ[:], LQ[:], ACT.Exp, scale=-0.5).then_inc(invq_ready, 1)

            def rstd(k):
                if known(k, PAIRS):
                    need(act, mv2_ready, k + 1)
                    a.activation(lnv2[:], mv2[:, 1:2], ACT.Ln, bias=eps[:, 0:1]).then_inc(lnv2_ready, 1)
                    need(act, lnv2_ready, k + 1)
                    a.activation(rstd2[:], lnv2[:], ACT.Exp, scale=-0.5).then_inc(rstd2_ready, 1)

            def modulate(k):
                if known(k, PAIRS):
                    need(act, xt2_ready, k + 1)
                    b = k // PB
                    a.activation(H2[:], pT, ACT.Identity, bias=mod[:, 3, bass.ds(b, 1)],
                                 scale=mod[:, 4, bass.ds(b, 1)]).then_inc(h2_ready, 1)

            def body(i):
                left_out(2 * i - 2, 0)
                denominator(i - 2)
                distance(2 * i - 1, 1)
                weigh(2 * i - 2, 0)
                scores(2 * i, 0)
                rstd(i - 3)
                weights_t(2 * i - 2, 0)
                values(2 * i - 2, 0)
                modulate(i - 3)
                left_out(2 * i - 1, 1)
                query_norm(i - 1)
                distance(2 * i, 0)
                weigh(2 * i - 1, 1)
                scores(2 * i + 1, 1)
                weights_t(2 * i - 1, 1)
                values(2 * i - 1, 1)

            run(act, body)

        @block.vector
        def _(dve):
            v = nc.vector
            steps = [0]

            def done(ins):
                steps[0] += 1
                ins.then_inc(dve_step, 1)
                return steps[0]

            def then(ins):
                dve.wait_ge(dve_step, done(ins))

            for c, e in enumerate((1e-5, 1e-8, 1e-18, LEFT_OUT)):
                last = v.memset(eps[:, c:c + 1], e)
            done(last)
            dve.wait_ge(act_step, 1)
            then(v.tensor_scalar(silu_c[:, 1], silu_c[:, 0], 1.0, None, ALU.add))
            then(v.reciprocal(silu_c[:, 2], silu_c[:, 1]))
            then(v.scalar_tensor_tensor(bb[:, 1:2], we("b2"), 0.1, we("base"), ALU.mult, ALU.add))
            then(v.tensor_tensor(silu_c[:, 3], silu_c[:, 2], we("c_t"), ALU.mult))
            for b in range(B):
                last = v.tensor_copy(silu_rows[:, b], silu_c[:, 3, b:b + 1].to_broadcast([P, P]))
            done(last)
            def moments(b):
                dve.wait_ge(x_loaded[b], 16)
                for k in range(b * PB, (b + 1) * PB):
                    last = v.bn_stats(stats1[:, k], X[:, k])
                then(last)
                for k in range(b * PB, (b + 1) * PB):
                    last = v.bn_aggr(mv1[:, k], stats1[:, k])
                last.then_inc(stats1_ready, 1)

            moments(0)
            dve.wait_ge(pe_step, 1)
            pm = bank[2][:, 0:6 * B].rearrange("p (j b) -> p j b", b=B)
            for j, add in ((0, 0.0), (1, 1.0), (3, 0.0), (4, 1.0)):
                last = v.tensor_scalar(mod[:, j], pm[:, j], add, None, ALU.add)
            last.then_inc(mod_ready, 1)
            dve.wait_ge(consts_loaded, 16)
            v.tensor_copy(ident_b[:], ident)
            done(v.tensor_copy(window_b[:], co("window")))
            for w in range(B * UNITS):
                b = w // UNITS
                if w == 1:
                    moments(1)
                if w % UNITS == 0:
                    dve.wait_ge(rstd1_ready, b + 1)
                need(dve, xt1_ready, w - 1)
                for k in range(w * UT, (w + 1) * UT):
                    ins = v.tensor_scalar(XN1[:, w % 2, (k % UT) * P:(k % UT + 1) * P], X[:, k],
                                          mv1[:, k, 0:1], rstd1[:, k:k + 1], ALU.subtract, ALU.mult)
                ins.then_inc(xn1_ready, 1)
            for b in range(B):
                dve.wait_ge(q_ready, (b + 1) * UNITS)
                v.tensor_reduce(esum[:, b:b + 1], Q[:, b * TP:b * TP + T].rearrange("p (n e) -> p n e", e=8)[:, :, 7],
                                AX, ALU.add).then_inc(e_summed, 1)
            dve.wait_ge(e_summed, B)
            then(v.tensor_reduce(sig[:, 0], qsum[:], AX, ALU.add))
            then(v.tensor_scalar(sig[:, 0], sig[:, 0], 1.0 / T, None, ALU.mult))
            done(v.scalar_tensor_tensor(sig[:, 2], esum[:], 0.5 / (T // 8), sig[:, 0], ALU.mult, ALU.add))
            dve.wait_ge(act_step, 4)
            v.tensor_scalar(gate_sign[:], bank[3][:, :].rearrange("p (j b d) -> p j b d", j=2, b=B), 0.0, 2.0,
                            ALU.is_ge, ALU.mult)
            then(v.tensor_scalar(gate_abs[:], gate_abs[:], 0.25, None, ALU.max))
            then(v.scalar_tensor_tensor(gates[:], gate_sign[:], -1.0, gate_abs[:], ALU.add, ALU.mult))
            r32 = NH * RANK
            done(v.tensor_tensor(
                UB[:], we("u_t")[0:r32, :].rearrange("p (h d) -> p h d", h=1).to_broadcast([r32, NH, HD]),
                co("head_r")[0:r32, :].rearrange("p (h d) -> p h d", d=1).to_broadcast([r32, NH, HD]), ALU.mult))
            dve.wait_ge(pe_step, 3)
            v.tensor_copy(R1T[:], bank[4][:, 0:D])
            done(v.tensor_copy(R2T[:], bank[4][:, D:2 * D]))
            dve.wait_ge(pe_step, 6)
            for b in range(B):
                v.tensor_tensor(DEC[:, b], we("decoder"), gates[:, 0, b], ALU.mult)
                v.tensor_tensor(FF[:, b], bank[5][:, 0:D], gates[:, 1, b], ALU.mult)
                v.tensor_tensor(FB[:, b], we("bias"), gates[:, 1, b], ALU.mult)
            v.tensor_tensor(HEB[:], bank[6][:, 0:HD].rearrange("p (h d) -> p h d", h=1).to_broadcast([P, NH, HD]),
                            co("head").rearrange("p (h d) -> p h d", d=1).to_broadcast([P, NH, HD]), ALU.mult)
            dve.wait_ge(act_step, 9)
            then(v.scalar_tensor_tensor(met[:, 4], met[:, 0], 0.0, met[:, 3], ALU.max, ALU.add))
            dve.wait_ge(pool_step, 3 * B)
            for b in range(B):
                v.tensor_scalar(HM2[:, b], co("head"), met[:, 4, b:b + 1], 2.0, ALU.mult, ALU.mult)
                last = v.tensor_scalar(QM2[:, b * TP:(b + 1) * TP], Q2[:, b * TP:(b + 1) * TP],
                                       met[:, 4, b:b + 1], None, ALU.mult)
            last.then_inc(setup_done, 1)
            dve.wait_ge(setup_done, 1)
            dve.wait_ge(cleared, 3)

            def own_scores(n, u):
                if known(n, 2 * PAIRS):
                    need(dve, scores_copied, n + 1)
                    v.tensor_tensor(DG[:, u], S[:, u, :, 0:BLK],
                                    co("diag").rearrange("p (k t) -> p k t", k=1).to_broadcast([P, GB, BLK]),
                                    ALU.mult).then_inc(diag_masked[u], 1)

            def own_sums(n, u):
                if known(n, 2 * PAIRS):
                    dve.wait_ge(diag_masked[u], 1)
                    v.tensor_reduce(SELF[:, u], DG[:, u], AX, ALU.add).then_inc(self_ready, 1)

            def take8(r, u):
                src = R if r else S
                for k in range(GB):
                    if r:
                        dve.wait_ge(marked, GB * (r - 1) + k + 1)
                    v.max(top8[:, k], src[:, u, k]).then_inc(top8_found, 1)
                for k in range(GB):
                    dve.wait_ge(top8_found, GB * r + k + 1)
                    v.match_replace(R[:, u, k], top8[:, k], src[:, u, k], TAKEN).then_inc(marked, 1)

            def end_group(n, u):
                if known(n, 2 * PAIRS):
                    dve.wait_ge(marked, GB * ROUNDS)
                    dve.sem_clear(marked)
                    dve.sem_clear(top8_found)
                    dve.sem_clear(stats2_found)
                    dve.sem_clear(diag_masked[u])
                    dve.sem_inc(group_taken)

            def normalise(k):
                if known(k, PAIRS):
                    need(dve, rden_ready, k + 1)
                    v.tensor_tensor(CN[:], pC, RD[:], ALU.mult).then_inc(cn_ready, 1)

            def gate(k):
                if known(k, PAIRS):
                    need(dve, invq_ready, k + 1)
                    v.scalar_tensor_tensor(G0[:], pN, 0.04, IQ[:], ALU.is_gt, ALU.mult).then_inc(gate_ready, 1)

            def residual(k):
                if known(k, PAIRS):
                    need(dve, att_ready, k + 1)
                    v.tensor_tensor(X1[:], pA, X[:, bass.ds(k, 1), :], ALU.add).then_inc(x1_ready, 1)

            def moments(k):
                if known(k, PAIRS):
                    need(dve, x1_ready, k + 1)
                    v.bn_stats(stats2[:], X1[:]).then_inc(stats2_found, 1)

            def moments_out(k):
                if known(k, PAIRS):
                    dve.wait_ge(stats2_found, 1)
                    v.bn_aggr(mv2[:], stats2[:]).then_inc(mv2_ready, 1)

            def normed(k):
                if known(k, PAIRS):
                    need(dve, rstd2_ready, k + 1)
                    v.tensor_scalar(XN2[:], X1[:], mv2[:, 0:1], rstd2[:], ALU.subtract,
                                    ALU.mult).then_inc(xn2_ready, 1)

            def result(k):
                if known(k, PAIRS):
                    need(dve, y_ready, k + 1)
                    need(dve, stored, 16 * k)
                    v.tensor_tensor(OUT[:], pY, X1[:], ALU.add).then_inc(out_ready, 1)

            def body(i):
                more = known(i, PAIRS)
                for u in range(2):
                    n = 2 * i + u
                    own_scores(n, u)
                    end_group(n - 1, 1 - u)
                    if u == 1:
                        moments(i - 2)
                    own_sums(n, u)
                    if more:
                        take8(0, u)
                    if u == 0:
                        result(i - 3)
                    else:
                        gate(i - 1)
                        moments_out(i - 2)
                    if more:
                        take8(1, u)
                    if u == 1:
                        normalise(i - 1)
                    if more:
                        take8(2, u)
                    if u == 0:
                        residual(i - 2)
                    else:
                        normed(i - 2)
                    if more:
                        take8(3, u)
                    if not more and u:
                        dve.drain()
                        dve.sem_clear(stats2_found)

            run(dve, body)

        @block.tensor
        def _(pe):
            t = nc.tensor
            pe.wait_ge(weights_loaded, 16)
            pe.wait_ge(dve_step, 6)
            for j in range(6):
                last = t.matmul(bank[2][:, j * B:(j + 1) * B], we("wmod")[:, j * D:(j + 1) * D], silu_c[:, 3],
                                start=True, stop=True)
            last.then_inc(pe_step, 1)
            for n, j in enumerate((2, 5)):
                for b in range(B):
                    at = (n * B + b) * D
                    last = t.matmul(bank[3][:, at:at + D], silu_rows[:, b], we("wmod")[:, j * D:(j + 1) * D],
                                    start=True, stop=True)
            last.then_inc(pe_step, 1)
            pe.wait_ge(consts_loaded, 16)
            for n, (w0, m0, w1, m1) in enumerate((("w_re", "cos", "w_im", "sin"), ("w_im", "cos", "w_re", "msin"))):
                o = bank[4][:, n * D:(n + 1) * D]
                t.matmul(o, we(w0), co(m0), start=True, stop=False)
                last = t.matmul(o, we(w1), co(m1), start=False, stop=True)
            last.then_inc(pe_step, 1)
            def turned(w):
                pe.wait_ge(xn1_ready, w + 1)
                need(pe, h_ready, w - 1)
                for c in range(UT):
                    last = t.transpose(bank[w % 2][:, c * P:(c + 1) * P], XN1[:, w % 2, c * P:(c + 1) * P], ident)
                last.then_inc(xt1_ready, 1)

            turned(0)
            for w in range(B * UNITS):
                if w + 1 < B * UNITS:
                    turned(w + 1)
                pe.wait_ge(h_ready, w + 1)
                need(pe, q_ready, w - 1)
                t.matmul(bank[6 + w % 2][:, :], we("enc_q"), HT[:, unit_cols(w)],
                         start=True, stop=True).then_inc(qmm_ready, 1)
            pe.wait_ge(dve_step, 15)
            pe.wait_ge(q_ready, B * UNITS)
            r32 = NH * RANK
            t.matmul(bank[6][:, 0:HD], UB[:].rearrange("p h d -> p (h d)"), we("v")[0:r32, :],
                     start=True, stop=True).then_inc(pe_step, 1)
            pe.wait_ge(dve_step, 16)
            t.matmul(bank[5][:, 0:D], R1T[:], co("cos_n"), start=True, stop=False).then_inc(pe_step, 1)
            t.matmul(bank[5][:, 0:D], R2T[:], co("msin_n"), start=False, stop=True).then_inc(pe_step, 1)
            t.matmul(bank[2][0:MLP, 0:B], we("w1"), sig[:, 2], start=True, stop=True).then_inc(pe_step, 1)
            pe.wait_ge(act_step, 5)
            t.matmul(bank[2][:, 0:B], we("w2")[0:MLP, :], mlp[:], start=True, stop=True).then_inc(pe_step, 1)
            pe.wait_ge(setup_done, 1)
            pe.wait_ge(pool_step, 3 * B)

            def scores(i, u):
                n = 2 * i + u
                if known(n, 2 * PAIRS):
                    need(pe, expanded, n + 1)
                    need(pe, scores_copied, n - 1)
                    own = QM2[:, bass.ds(column(i, u), P)]
                    spans = bass.AP(tensor=own.tensor, offset=own.offset,
                                    ap=[list(own.ap[0]), [BLK, GB], [1, SPAN]])
                    t.matmul(pS[u], co("minus_head"), spans, start=True, stop=False)
                    t.matmul(pS[u], ident_b[:], window_b[:].rearrange("p (k j) -> p k j", k=1).to_broadcast([P, GB, SPAN]),
                             start=False, stop=False)
                    for k in range(GB):
                        keys = bass.ds(column(i, u) + k * BLK, SPAN)
                        last = t.matmul(pS[u][:, k], A[:, u, k].rearrange("p h t -> p (h t)"), Q[:, keys],
                                        start=False, stop=(k == GB - 1))
                    last.then_inc(scores_ready, 1)

            def values(i, u):
                n = 2 * i + u
                if known(n, 2 * PAIRS):
                    need(pe, v_copied, n)
                    need(pe, frame_copied, n + 1)
                    t.matmul(pV, HV[:, u], we("enc_v"), start=True,
                             stop=True).then_inc(v_ready, 1)

            def weights_t(n, u):
                if known(n, 2 * PAIRS):
                    need(pe, weights_ready, n + 1)
                    need(pe, wt_copied, n - 1)
                    for k in range(GB):
                        last = t.transpose(pW[u][:, k], W[:, u, k], ident)
                    last.then_inc(wt_ready, 1)

            def context(i, u):
                n = 2 * i + u
                if known(n, 2 * PAIRS):
                    need(pe, wt_copied, n + 1)
                    need(pe, v_copied, n + 1)
                    need(pe, cn_ready, i)
                    ones = co("parity").rearrange("p (s c) -> p s c", s=2)
                    for dst, src in ((pC, None), (pD, ones)):
                        for a in range(4):
                            for s in range(2):
                                lhs = V[:, u, s, a * PQ:(a + 1) * PQ] if src is None else src[:, s, :]
                                last = t.matmul(dst[a * PQ:(a + 1) * PQ, u * GQ:(u + 1) * GQ], lhs,
                                                WT[:, u, :, 2 * a + s, :], start=(s == 0), stop=(s == 1))
                    last.then_inc(context_ready, 1)

            def norms(k):
                if known(k, PAIRS):
                    need(pe, heb_ready, k)
                    cols = bass.ds(column(k), P)
                    t.matmul(pN, co("same_head"), Q2[:, cols], start=True, stop=True)
                    t.matmul(pH, HEB[:].rearrange("p h d -> p (h d)"), Q[:, cols], start=True,
                             stop=True).then_inc(norms_ready, 1)

            def attention(k):
                if known(k, PAIRS):
                    need(pe, o_ready, k + 1)
                    need(pe, out_ready, k)
                    t.matmul(pA, O[:], DEC[:, bass.ds(k // PB, 1)].rearrange("p o d -> p (o d)"), start=True,
                             stop=True).then_inc(att_ready, 1)

            def normed_t(k):
                if known(k, PAIRS):
                    need(pe, xn2_ready, k + 1)
                    t.transpose(pT, XN2[:], ident).then_inc(xt2_ready, 1)

            def feed_forward(k):
                if known(k, PAIRS):
                    need(pe, h2_ready, k + 1)
                    b = bass.ds(k // PB, 1)
                    t.matmul(pY, H2[:], FF[:, b].rearrange("p o d -> p (o d)"), start=True, stop=False)
                    t.matmul(pY, co("row0"), FB[:, b].rearrange("p o d -> p (o d)"), start=False,
                             stop=True).then_inc(y_ready, 1)

            def body(i):
                scores(i, 0)
                weights_t(2 * i - 2, 0)
                values(i - 1, 0)
                context(i - 1, 0)
                normed_t(i - 3)
                norms(i - 1)
                feed_forward(i - 3)
                scores(i, 1)
                attention(i - 2)
                weights_t(2 * i - 1, 1)
                values(i - 1, 1)
                context(i - 1, 1)

            run(pe, body)


def _constants():
    import numpy as np
    c = np.zeros((P, CONST_W), np.float32)

    def put(name, value):
        a, w = CONST_COLS[name]
        value = np.asarray(value)
        c[:value.shape[0], a:a + w] = value

    p = np.arange(P)
    angle = 2 * np.pi * ((p[:, None] * p[None, :]) % D) / D
    put("ident", np.eye(P))
    put("cos", np.cos(angle))
    put("sin", np.sin(angle))
    put("msin", -np.sin(angle))
    put("cos_n", np.cos(angle) / D)
    put("msin_n", -np.sin(angle) / D)
    put("head", p[:, None] // HD == np.arange(NH)[None, :])
    put("same_head", p[:, None] // HD == p[None, :] // HD)
    q = p % BLK
    put("diag", q[:, None] == np.arange(BLK)[None, :])
    off = np.arange(SPAN)[None, :] - q[:, None]
    put("window", np.where((off >= 0) & (off < WINDOW), 0.0, OUTSIDE))
    put("parity", np.broadcast_to(np.arange(2 * PQ)[None, :] // PQ == (np.arange(2 * PQ)[None, :] % PQ) // HD, (P, 2 * PQ)))
    put("row0", np.broadcast_to(p[:, None] == 0, (P, P)))
    put("minus_head", -1.0 * (p[:, None] // HD == p[None, :] // BLK))
    put("head_r", np.arange(NH * RANK)[:, None] // RANK == np.arange(NH)[None, :])
    return c


def kernel(**inputs):
    import numpy as np
    import concourse.bacc as bacc
    from concourse.bass_utils import run_bass_kernel_spmd

    given = {k[3:]: np.asarray(a) for k, a in inputs.items()}
    w = np.zeros((P, WEIGHT_W), np.float32)
    for name, a in (
        ("c_t", given["c"].T), ("wmod", given["wmod"]),
        ("enc_q", given["attn_enc_q"].transpose(1, 0, 2).reshape(D, D)),
        ("enc_v", given["attn_enc_v"].transpose(1, 0, 2).reshape(D, D)),
        ("w1", given["attn_metric_w1"]), ("w2", given["attn_metric_w2"]),
        ("b1", given["attn_metric_b1"].reshape(-1, 1)), ("b2", given["attn_metric_b2"].reshape(-1, 1)),
        ("base", given["attn_base_metric"].reshape(-1, 1)),
        ("u_t", given["attn_hebb_U"].transpose(0, 2, 1).reshape(NH * RANK, HD)),
        ("v", given["attn_hebb_V"].reshape(NH * RANK, HD)),
        ("decoder", given["attn_decoder"]), ("w_re", given["ffn_w_freq_real"]),
        ("w_im", given["ffn_w_freq_imag"]), ("bias", given["ffn_bias"].reshape(1, D)),
    ):
        at, width = WEIGHT_COLS[name]
        w[:a.shape[0], at:at + width] = a
    arrays = {"x": np.ascontiguousarray(given["attn_x"][:, ::-1, :]), "weights": w, "consts": _constants()}

    nc = bacc.Bacc("TRN2", target_bir_lowering=False, num_devices=1)
    aps = [nc.dram_tensor(n, a.shape, F32, kind="ExternalInput").ap() for n, a in arrays.items()]
    aps.append(nc.dram_tensor("out", (B * T, D), F32, kind="ExternalOutput").ap())
    build(nc, *aps)
    r = run_bass_kernel_spmd(nc, [arrays], core_ids=[0])
    return np.ascontiguousarray(r.results[0]["out"].reshape(B, T, D)[:, ::-1, :])
```

```python
import concourse.bass as bass
from concourse import mybir
from contextlib import ExitStack

F32 = mybir.dt.float32
BF16 = mybir.dt.bfloat16
ALU = mybir.AluOpType
ACT = mybir.ActivationFunctionType
AX = mybir.AxisListType.X

B, T, D = 2, 2048, 128
NH, HD, RANK = 8, 16, 4
WINDOW, TOPK = 64, 32
MLP = 64
P = 128
BLK = P // NH
SPAN = BLK - 1 + WINDOW
GB = 4
GQ = GB * BLK
PAIRS = B * T // P
PB = T // P
PAD = WINDOW
TP = T + PAD
UNIT = 512
UNITS = T // UNIT
UT = UNIT // P
ROUNDS = TOPK // 8
OUTSIDE = -2.0 ** 60
LEFT_OUT = 1024.0
TAKEN = -2.0 ** 100
PQ = P // 4

CONST_COLS = {}
_at = 0
for _n, _w in (("ident", P), ("cos", P), ("sin", P), ("msin", P), ("cos_n", P), ("msin_n", P),
               ("head", NH), ("same_head", P), ("window", SPAN), ("parity", 2 * PQ),
               ("row0", P), ("head_r", NH), ("minus_head", P)):
    CONST_COLS[_n] = (_at, _w)
    _at += _w
CONST_W = _at
WEIGHT_COLS = {}
_at = 0
for _n, _w in (("c_t", B), ("wmod", 6 * D), ("enc_q", D), ("enc_v", D), ("w1", MLP), ("w2", D), ("b1", 1),
               ("b2", 1), ("base", 1), ("u_t", HD), ("v", HD), ("decoder", D), ("w_re", D),
               ("w_im", D), ("bias", D)):
    WEIGHT_COLS[_n] = (_at, _w)
    _at += _w
WEIGHT_W = _at


def build(nc, x, weights, consts, out):
    ctx = ExitStack()
    with ctx:
        def sb(name, shape, dt=F32):
            return ctx.enter_context(nc.sbuf_tensor(name, shape, dt))

        def sem(name):
            return ctx.enter_context(nc.semaphore(name))

        X = sb("X", [P, PAIRS, D])
        CO = sb("CO", [P, CONST_W])
        WE = sb("WE", [P, WEIGHT_W])

        def co(name):
            a, w = CONST_COLS[name]
            return CO[:, a:a + w]

        def we(name):
            a, w = WEIGHT_COLS[name]
            return WE[:, a:a + w]

        ident = co("ident")
        HT = sb("HT", [P, B * TP])
        Q = sb("Q", [P, B * TP])
        Q2 = sb("Q2", [P, B * TP])
        ident_b = sb("ident_b", [P, P], BF16)
        window_b = sb("window_b", [P, SPAN], BF16)
        XN1 = sb("XN1", [P, 2, UNIT])
        stats1 = sb("stats1", [P, PAIRS, 6])
        mv1 = sb("mv1", [P, PAIRS, 2])
        lnv1 = sb("lnv1", [P, PAIRS])
        rstd1 = sb("rstd1", [P, PAIRS])
        silu_c = sb("silu_c", [P, 4, B])
        silu_rows = sb("silu_rows", [P, B, P])
        mod = sb("mod", [P, 6, B])
        gates = sb("gates", [P, 2, B, D])
        gate_abs = sb("gate_abs", [P, 2, B, D])
        gate_sign = sb("gate_sign", [P, 2, B, D])
        DEC = sb("DEC", [P, B, D])
        R1T = sb("R1T", [P, D])
        R2T = sb("R2T", [P, D])
        FF = sb("FF", [P, B, D])
        FB = sb("FB", [P, B, D])
        UB = sb("UB", [NH * RANK, NH, HD])
        HEB = sb("HEB", [P, NH, HD])
        qsum = sb("qsum", [P, B, UNITS])
        sig = sb("sig", [P, 3, B])
        mlp = sb("mlp", [MLP, B])
        met = sb("met", [P, 6, B])
        bb = sb("bb", [P, 2])
        eps = sb("eps", [P, 4])
        HM2 = sb("HM2", [P, B, NH])
        QM2 = sb("QM2", [P, B * TP])
        HV = sb("HV", [P, 2, P])
        A = sb("A", [P, 2, GB, NH, BLK])
        S = sb("S", [P, 2, GB, SPAN])
        R = sb("R", [P, 2, GB, SPAN])
        first8 = sb("first8", [P, 2, GB, 8])
        Y = sb("Y", [P, 2, GB, SPAN])
        U = sb("U", [P, 2, GB, SPAN])
        top8 = sb("top8", [P, GB, 8])
        W = sb("W", [P, 2, GB, P])
        WT = sb("WT", [P, 2, GB, NH, BLK])
        V = sb("V", [P, 2, 2, P])
        DEN = sb("DEN", [P, P])
        LD = sb("LD", [P, P])
        RD = sb("RD", [P, P])
        CN = sb("CN", [P, P])
        ND = sb("ND", [P, 2, P])
        two = sb("two", [P, 1])
        CR = sb("CR", [P, P])
        LQ = sb("LQ", [P, P])
        IQ = sb("IQ", [P, P])
        QH = sb("QH", [P, P])
        G0 = sb("G0", [P, P])
        G = sb("G", [P, P])
        CG = sb("CG", [P, P])
        O = sb("O", [P, P])
        X1 = sb("X1", [P, D])
        stats2 = sb("stats2", [P, 6])
        mv2 = sb("mv2", [P, 2])
        lnv2 = sb("lnv2", [P, 1])
        rstd2 = sb("rstd2", [P, 1])
        minus_mean = sb("minus_mean", [P, 1])
        shift2 = sb("shift2", [P, 1])
        XN2 = sb("XN2", [P, D])
        H2 = sb("H2", [P, P])
        OUT = sb("OUT", [P, D])

        bank = [ctx.enter_context(nc.psum_tensor(f"bank{k}", [P, 512], F32)) for k in range(8)]
        pS = [bank[k][:, 0:GB * SPAN].rearrange("p (k j) -> p k j", k=GB) for k in range(2)]
        pW = [bank[2 + k][:, :].rearrange("p (k c) -> p k c", k=GB) for k in range(2)]
        pV = bank[4][:, 0:P]
        pC = bank[5][:, 0:P]
        pD = bank[6][:, 3 * P:4 * P]
        pN = bank[6][:, 0:P]
        pH = bank[6][:, P:2 * P]
        pA = bank[7][:, 0:P]
        pT = bank[7][:, P:2 * P]
        pY = bank[4][:, P:2 * P]

        x_loaded = [sem(f"x_loaded{w}") for w in range(B * UNITS)]
        weights_loaded = [sem(f"weights_loaded{k}") for k in range(2)]
        consts_loaded = [sem(f"consts_loaded{k}") for k in range(2)]
        cleared = sem("cleared")
        act_step = sem("act_step")
        dve_step = sem("dve_step")
        eps_ready = sem("eps_ready")
        silu_exp_ready = sem("silu_exp_ready")
        silu_ready = sem("silu_ready")
        mod_product = sem("mod_product")
        gate_product = sem("gate_product")
        mod_ready = sem("mod_ready")
        stats1_ready = sem("stats1_ready")
        rstd1_ready = sem("rstd1_ready")
        xn1_ready = sem("xn1_ready")
        xt1_ready = sem("xt1_ready")
        h_ready = sem("h_ready")
        qmm_ready = sem("qmm_ready")
        q_ready = sem("q_ready")
        q2_ready = sem("q2_ready")
        padded = sem("padded")
        signal_ready = sem("signal_ready")
        hidden_product = sem("hidden_product")
        hidden_ready = sem("hidden_ready")
        metric_product = sem("metric_product")
        softplus_ready = sem("softplus_ready")
        metric_ready = sem("metric_ready")
        key_norms_ready = sem("key_norms_ready")
        consts_b_ready = sem("consts_b_ready")
        gate_abs_ready = sem("gate_abs_ready")
        spectrum_product = sem("spectrum_product")
        spectrum_ready = sem("spectrum_ready")
        ff_product = sem("ff_product")
        ub_ready = sem("ub_ready")
        heb_product = sem("heb_product")
        setup_done = sem("setup_done")
        expanded = sem("expanded")
        scores_ready = sem("scores_ready")
        scores_copied = sem("scores_copied")
        first8_ready = sem("first8_ready")
        dist2_ready = sem("dist2_ready")
        chain = sem("chain")
        group_taken = sem("group_taken")
        left_out_ready = sem("left_out_ready")
        exponent_ready = sem("exponent_ready")
        weights_ready = sem("weights_ready")
        wt_ready = sem("wt_ready")
        wt_copied = sem("wt_copied")
        frame_copied = sem("frame_copied")
        v_ready = sem("v_ready")
        v_copied = sem("v_copied")
        context_ready = sem("context_ready")
        stats2_found = sem("stats2_found")
        top8_found = sem("top8_found")
        marked = sem("marked")
        den_summed = sem("den_summed")
        den_ready = sem("den_ready")
        lnden_ready = sem("lnden_ready")
        rden_ready = sem("rden_ready")
        cn_ready = sem("cn_ready")
        norms_ready = sem("norms_ready")
        lnq_ready = sem("lnq_ready")
        invq_ready = sem("invq_ready")
        qh_copied = sem("qh_copied")
        gate_ready = sem("gate_ready")
        heb_ready = sem("heb_ready")
        newton_step = sem("newton_step")
        o_ready = sem("o_ready")
        att_ready = sem("att_ready")
        x1_copied = sem("x1_copied")
        mv2_ready = sem("mv2_ready")
        lnv2_ready = sem("lnv2_ready")
        rstd2_ready = sem("rstd2_ready")
        minus_mean_ready = sem("minus_mean_ready")
        shift2_ready = sem("shift2_ready")
        xn2_ready = sem("xn2_ready")
        xt2_ready = sem("xt2_ready")
        h2_ready = sem("h2_ready")
        y_ready = sem("y_ready")
        out_ready = sem("out_ready")
        stored = sem("stored")

        LAG = 2

        def need(eng, s, value):
            if not isinstance(value, int) or value > 0:
                eng.wait_ge(s, value)

        def known(k, count):
            return not isinstance(k, int) or 0 <= k < count

        def column(i, u=0):
            return i * P + (i // PB) * PAD + u * GQ

        def run(eng, body):
            for i in range(LAG):
                body(i)
            with eng.Fori(LAG, PAIRS - 1) as i:
                body(i)
            for i in range(PAIRS - 1, PAIRS + LAG):
                body(i)

        AHEAD = UNITS + 1

        def unit_cols(w):
            at = (w // UNITS) * TP + (w % UNITS) * UNIT
            return slice(at, at + UNIT)

        block = ctx.enter_context(nc.Block())

        @block.sync
        def _(sp):
            for w in range(B * UNITS):
                rows = x[w // UNITS, (w % UNITS) * UNIT:(w % UNITS + 1) * UNIT, :]
                sp.dma_start(X[:, w * UT:(w + 1) * UT, :],
                             rows.rearrange("(k p) d -> p k d", p=P)).then_inc(x_loaded[w], 16)

            def store(i):
                k = i - 2
                if known(k, PAIRS):
                    need(sp, out_ready, k + 1)
                    sp.dma_start(out[bass.ds(k * P, P), :], OUT[:, :]).then_inc(stored, 16)

            run(sp, store)
            sp.wait_ge(stored, 16 * PAIRS)

        @block.gpsimd
        def _(pool):
            g = nc.gpsimd
            g.memset(W[:], 0.0).then_inc(cleared, 1)
            g.memset(V[:], 0.0).then_inc(cleared, 1)
            g.memset(two[:], 2.0).then_inc(cleared, 1)

            def squares(w):
                pool.wait_ge(q_ready, w + 1)
                g.tensor_tensor(Q2[:, unit_cols(w)], Q[:, unit_cols(w)], Q[:, unit_cols(w)],
                                ALU.mult).then_inc(q2_ready, 1)
                if w % UNITS == UNITS - 1:
                    pool.wait_ge(q2_ready, w + 1)
                    last = (w // UNITS) * TP + T
                    for arr in (HT, Q, Q2):
                        g.tensor_copy(arr[:, last:last + PAD],
                                      arr[:, last - 1:last].to_broadcast([P, PAD])).then_inc(padded, 1)

            def expand(i, u):
                n = 2 * i + u
                if known(n, 2 * PAIRS):
                    need(pool, scores_ready, n - 1)
                    q = Q[:, bass.ds(column(i, u), GQ)].rearrange("p (k h t) -> p k h t", k=GB, h=1)
                    m = HM2[:, (i // PB), :].rearrange("p (k h t) -> p k h t", k=1, t=1)
                    g.tensor_tensor(A[:, u], q.to_broadcast([P, GB, NH, BLK]),
                                    m.to_broadcast([P, GB, NH, BLK]), ALU.mult).then_inc(expanded, 1)

            def frame(i, u):
                n = 2 * i + u
                if known(n, 2 * PAIRS):
                    need(pool, v_ready, n - 1)
                    g.tensor_copy(HV[:, u], HT[:, bass.ds(column(i, u), P)]).then_inc(frame_copied, 1)

            def distance(n, u):
                if known(n, 2 * PAIRS):
                    need(pool, first8_ready, n + 1)
                    g.tensor_tensor(Y[:, u], first8[:, u, :, 0:1].to_broadcast([P, GB, SPAN]),
                                    S[:, u], ALU.subtract).then_inc(dist2_ready, 1)

            def exponent(n, u):
                if known(n, 2 * PAIRS):
                    need(pool, left_out_ready, n + 1)
                    g.tensor_tensor(Y[:, u], Y[:, u], U[:, u], ALU.add).then_inc(exponent_ready, 1)

            def refined(k):
                if known(k, PAIRS):
                    need(pool, den_ready, k + 1)
                    g.tensor_tensor(ND[:, 0], DEN[:], RD[:], ALU.mult).then_inc(newton_step, 1)
                    need(pool, newton_step, 4 * k + 1)
                    g.tensor_tensor(ND[:, 1], two[:, 0:1].to_broadcast([P, P]), ND[:, 0],
                                    ALU.subtract).then_inc(newton_step, 1)

            def scaled(k):
                if known(k, PAIRS):
                    need(pool, newton_step, 4 * k + 2)
                    need(pool, cn_ready, k + 1)
                    g.tensor_tensor(CR[:], CN[:], ND[:, 1], ALU.mult).then_inc(newton_step, 1)

            def gated(k):
                if known(k, PAIRS):
                    need(pool, newton_step, 4 * k + 3)
                    need(pool, heb_ready, k + 1)
                    g.tensor_tensor(CG[:], CR[:], G[:], ALU.add).then_inc(newton_step, 1)
                    need(pool, newton_step, 4 * k + 4)
                    need(pool, att_ready, k)
                    g.tensor_tensor(O[:], CG[:], Q[:, bass.ds(column(k), P)], ALU.mult).then_inc(o_ready, 1)

            def hebbian(k):
                if known(k, PAIRS):
                    need(pool, gate_ready, k + 1)
                    need(pool, qh_copied, k + 1)
                    need(pool, o_ready, k)
                    g.tensor_tensor(G[:], G0[:], QH[:], ALU.mult).then_inc(heb_ready, 1)

            def body(i):
                exponent(2 * i - 1, 1)
                distance(2 * i, 0)
                expand(i + 1, 0)
                if isinstance(i, int) and i == 0:
                    for w in range(AHEAD, B * UNITS):
                        squares(w)
                frame(i, 0)
                frame(i, 1)
                refined(i - 1)
                scaled(i - 1)
                exponent(2 * i, 0)
                distance(2 * i + 1, 1)
                gated(i - 1)
                hebbian(i)
                expand(i + 1, 1)

            for w in range(AHEAD):
                squares(w)
            pool.wait_ge(metric_ready, 1)
            pool.wait_ge(cleared, 3)
            expand(0, 0)
            expand(0, 1)
            run(pool, body)

        @block.scalar
        def _(act):
            a = nc.scalar
            early_w, early_c = WEIGHT_COLS["enc_v"][0], CONST_COLS["cos"][0]
            act.dma_start(WE[:, 0:early_w], weights[:, 0:early_w]).then_inc(weights_loaded[0], 16)
            act.dma_start(CO[:, 0:early_c], consts[:, 0:early_c]).then_inc(consts_loaded[0], 16)
            act.dma_start(CO[:, early_c:], consts[:, early_c:]).then_inc(consts_loaded[1], 16)
            act.dma_start(WE[:, early_w:], weights[:, early_w:]).then_inc(weights_loaded[1], 16)
            steps = [0]

            def then(ins):
                steps[0] += 1
                ins.then_inc(act_step, 1)
                act.wait_ge(act_step, steps[0])

            TABLE = "natural_log_exp_and_others"
            a.preload_act_table_set(TABLE)
            act.wait_ge(weights_loaded[0], 16)
            a.activation(silu_c[:, 0], we("c_t"), ACT.Exp, scale=-1.0).then_inc(silu_exp_ready, 1)

            def rstd_unit(w):
                tiles = slice(w * UT, (w + 1) * UT)
                act.wait_ge(stats1_ready, w + 1)
                then(a.activation(lnv1[:, tiles], mv1[:, tiles, 1], ACT.Ln, bias=eps[:, 0:1]))
                a.activation(rstd1[:, tiles], lnv1[:, tiles], ACT.Exp, scale=-0.5).then_inc(rstd1_ready, 1)

            def modulated(w):
                b = w // UNITS
                act.wait_ge(xt1_ready, w + 1)
                a.activation(HT[:, unit_cols(w)], bank[w % 2][:, :], ACT.Identity,
                             bias=mod[:, 0, b:b + 1], scale=mod[:, 1, b:b + 1]).then_inc(h_ready, 1)

            def queries(w):
                act.wait_ge(qmm_ready, w + 1)
                a.activation(Q[:, unit_cols(w)], bank[6 + w % 2][:, :], ACT.Relu,
                             accum_out=qsum[:, w // UNITS, w % UNITS:w % UNITS + 1]).then_inc(q_ready, 1)

            def scores(n, u):
                if known(n, 2 * PAIRS):
                    need(act, scores_ready, n + 1)
                    a.activation(S[:, u], pS[u], ACT.Copy).then_inc(scores_copied, 1)

            def hidden(b):
                act.wait_ge(hidden_product, b + 1)
                a.activation(mlp[:, b:b + 1], bank[2][0:MLP, 16:17], ACT.Gelu,
                             bias=we("b1")[0:MLP, :]).then_inc(hidden_ready, 1)
                a.preload_act_table_set(TABLE)

            def softplus(b):
                act.wait_ge(metric_product, b + 1)
                then(a.activation(met[:, 0, b:b + 1], bank[2][:, 18:19], ACT.Identity, bias=bb[:, 1:2], scale=0.1))
                then(a.activation(met[:, 1, b:b + 1], met[:, 0, b:b + 1], ACT.Abs))
                then(a.activation(met[:, 2, b:b + 1], met[:, 1, b:b + 1], ACT.Exp, scale=-1.0))
                a.activation(met[:, 3, b:b + 1], met[:, 2, b:b + 1], ACT.Ln, bias=1.0).then_inc(softplus_ready, 1)

            act.wait_ge(eps_ready, 1)
            rstd_unit(0)
            rstd_unit(1)
            act.wait_ge(mod_ready, 1)
            modulated(0)
            for w in range(B * UNITS):
                if w + 2 < B * UNITS:
                    rstd_unit(w + 2)
                if w + 1 == B * UNITS - 1:
                    scores(0, 0)
                if w + 1 < B * UNITS:
                    modulated(w + 1)
                queries(w)
                if w == UNITS:
                    act.wait_ge(consts_b_ready, 1)
                    hidden(0)
                    softplus(0)
                if w == UNITS - 1:
                    act.wait_ge(gate_product, 1)
                    a.activation(gate_abs[:], bank[3][:, :], ACT.Abs).then_inc(gate_abs_ready, 1)

            def positive(n, u):
                if known(n, 2 * PAIRS):
                    need(act, dist2_ready, n + 1)
                    a.activation(Y[:, u], Y[:, u], ACT.Relu).then_inc(chain, 1)

            def ln_distance(n, u):
                if known(n, 2 * PAIRS):
                    need(act, chain, 2 * n + 1)
                    a.activation(Y[:, u], Y[:, u], ACT.Ln, bias=eps[:, 1:2]).then_inc(chain, 1)

            def distance(n, u):
                if known(n, 2 * PAIRS):
                    need(act, chain, 2 * n + 2)
                    a.activation(Y[:, u], Y[:, u], ACT.Exp, scale=0.5)

            def left_out(n, u):
                if known(n, 2 * PAIRS):
                    need(act, group_taken, n + 1)
                    a.activation(U[:, u], R[:, u], ACT.Relu, bias=eps[:, 3:4],
                                 scale=LEFT_OUT / -OUTSIDE).then_inc(left_out_ready, 1)

            def weigh(n, u):
                if known(n, 2 * PAIRS):
                    need(act, exponent_ready, n + 1)
                    need(act, wt_ready, n - 1)
                    w = W[:, u]
                    frame = bass.AP(tensor=w.tensor, offset=w.offset,
                                    ap=[list(w.ap[0]), [P + BLK, GB], [1, SPAN]])
                    a.activation(frame, Y[:, u], ACT.Exp, scale=-1.0).then_inc(weights_ready, 1)

            def values(n, u):
                if known(n, 2 * PAIRS):
                    need(act, v_ready, n + 1)
                    need(act, context_ready, n - 1)
                    dst = V[:, u].rearrange("p s (a s2 d) -> p a s s2 d", s2=2, d=HD)
                    for s in range(2):
                        ins = a.activation(dst[:, :, s, s, :],
                                           pV.rearrange("p (a s d) -> p a s d", s=2, d=HD)[:, :, s, :], ACT.Relu)
                    ins.then_inc(v_copied, 1)

            def weights_t(n, u):
                if known(n, 2 * PAIRS):
                    need(act, wt_ready, n + 1)
                    need(act, context_ready, n - 1)
                    a.activation(WT[:, u], pW[u], ACT.Copy).then_inc(wt_copied, 1)

            def denominator(k):
                if known(k, PAIRS):
                    need(act, den_summed, 2 * k + 2)
                    a.activation(LD[:], pD, ACT.Ln, bias=eps[:, 1:2]).then_inc(lnden_ready, 1)
                    need(act, lnden_ready, k + 1)
                    a.activation(RD[:], LD[:], ACT.Exp, scale=-1.0).then_inc(rden_ready, 1)
                    a.activation(DEN[:], pD, ACT.Identity, bias=eps[:, 1:2]).then_inc(den_ready, 1)

            def query_norm(k):
                if known(k, PAIRS):
                    need(act, norms_ready, k + 1)
                    a.activation(LQ[:], pN, ACT.Ln, bias=eps[:, 2:3]).then_inc(lnq_ready, 1)
                    a.activation(QH[:], pH, ACT.Copy, scale=0.1).then_inc(qh_copied, 1)
                    need(act, lnq_ready, k + 1)
                    a.activation(IQ[:], LQ[:], ACT.Exp, scale=-0.5).then_inc(invq_ready, 1)

            def rstd(k):
                if known(k, PAIRS):
                    need(act, mv2_ready, k + 1)
                    a.activation(lnv2[:], mv2[:, 1:2], ACT.Ln, bias=eps[:, 0:1]).then_inc(lnv2_ready, 1)
                    a.activation(minus_mean[:], mv2[:, 0:1], ACT.Copy, scale=-1.0).then_inc(minus_mean_ready, 1)
                    need(act, lnv2_ready, k + 1)
                    a.activation(rstd2[:], lnv2[:], ACT.Exp, scale=-0.5).then_inc(rstd2_ready, 1)

            def shift(k):
                if known(k, PAIRS):
                    need(act, minus_mean_ready, k + 1)
                    need(act, rstd2_ready, k + 1)
                    a.activation(shift2[:], minus_mean[:], ACT.Copy, scale=rstd2[:]).then_inc(shift2_ready, 1)

            def normed(k):
                if known(k, PAIRS):
                    need(act, shift2_ready, k + 1)
                    a.activation(XN2[:], X1[:], ACT.Identity, bias=shift2[:], scale=rstd2[:]).then_inc(xn2_ready, 1)

            def modulate(k):
                if known(k, PAIRS):
                    need(act, xt2_ready, k + 1)
                    b = k // PB
                    a.activation(H2[:], pT, ACT.Identity, bias=mod[:, 3, bass.ds(b, 1)],
                                 scale=mod[:, 4, bass.ds(b, 1)]).then_inc(h2_ready, 1)

            def result(k):
                if known(k, PAIRS):
                    need(act, y_ready, k + 1)
                    need(act, stored, 16 * k)
                    a.activation(OUT[:], pY, ACT.Copy).then_inc(out_ready, 1)

            def residual(k):
                if known(k, PAIRS):
                    need(act, att_ready, k + 1)
                    need(act, y_ready, k)
                    a.activation(X1[:], pA, ACT.Copy).then_inc(x1_copied, 1)

            def body(i):
                left_out(2 * i - 1, 1)
                rstd(i - 2)
                values(2 * i - 1, 1)
                shift(i - 2)
                weigh(2 * i - 1, 1)
                normed(i - 2)
                positive(2 * i, 0)
                weights_t(2 * i - 1, 1)
                scores(2 * i + 1, 1)
                modulate(i - 2)
                denominator(i - 1)
                ln_distance(2 * i, 0)
                result(i - 2)
                distance(2 * i, 0)
                if isinstance(i, int) and i == 0:
                    hidden(1)
                    softplus(1)
                left_out(2 * i, 0)
                query_norm(i)
                values(2 * i, 0)
                weigh(2 * i, 0)
                scores(2 * i + 2, 0)
                weights_t(2 * i, 0)
                positive(2 * i + 1, 1)
                ln_distance(2 * i + 1, 1)
                residual(i - 1)
                distance(2 * i + 1, 1)

            act.wait_ge(cleared, 2)
            run(act, body)

        @block.vector
        def _(dve):
            v = nc.vector
            steps = [0]

            def then(ins):
                steps[0] += 1
                ins.then_inc(dve_step, 1)
                dve.wait_ge(dve_step, steps[0])

            for c, e in enumerate((1e-5, 1e-8, 1e-18, LEFT_OUT)):
                last = v.memset(eps[:, c:c + 1], e)
            last.then_inc(eps_ready, 1)

            def moments1(w):
                dve.wait_ge(x_loaded[w], 16)
                for k in range(w * UT, (w + 1) * UT):
                    last = v.bn_stats(stats1[:, k], X[:, k])
                then(last)
                for k in range(w * UT, (w + 1) * UT):
                    last = v.bn_aggr(mv1[:, k], stats1[:, k])
                last.then_inc(stats1_ready, 1)

            def normed1(w):
                dve.wait_ge(rstd1_ready, w + 1)
                need(dve, xt1_ready, w - 1)
                for k in range(w * UT, (w + 1) * UT):
                    ins = v.tensor_scalar(XN1[:, w % 2, (k % UT) * P:(k % UT + 1) * P], X[:, k],
                                          mv1[:, k, 0:1], rstd1[:, k:k + 1], ALU.subtract, ALU.mult)
                ins.then_inc(xn1_ready, 1)

            def signal(b):
                dve.wait_ge(q_ready, (b + 1) * UNITS)
                v.tensor_reduce(sig[:, 0, b:b + 1], qsum[:, b:b + 1], AX, ALU.add)
                then(v.tensor_reduce(sig[:, 1, b:b + 1],
                                     Q[:, b * TP:b * TP + T].rearrange("p (n e) -> p n e", e=8)[:, :, 7], AX, ALU.add))
                then(v.tensor_scalar(sig[:, 0, b:b + 1], sig[:, 0, b:b + 1], 1.0 / T, None, ALU.mult))
                v.scalar_tensor_tensor(sig[:, 2, b:b + 1], sig[:, 1, b:b + 1], 0.5 / (T // 8), sig[:, 0, b:b + 1],
                                       ALU.mult, ALU.add).then_inc(signal_ready, 1)

            def metric(b):
                dve.wait_ge(softplus_ready, b + 1)
                then(v.scalar_tensor_tensor(met[:, 4, b:b + 1], met[:, 0, b:b + 1], 0.0, met[:, 3, b:b + 1],
                                            ALU.max, ALU.add))
                v.tensor_scalar(HM2[:, b], co("head"), met[:, 4, b:b + 1], 2.0, ALU.mult,
                                ALU.mult).then_inc(metric_ready, 1)
                dve.wait_ge(q2_ready, b * UNITS + 1)
                key_norms(b, 0, UNIT)

            def key_norms(b, start, end):
                part = slice(b * TP + start, b * TP + end)
                v.tensor_scalar(QM2[:, part], Q2[:, part], met[:, 4, b:b + 1], None,
                                ALU.mult).then_inc(key_norms_ready, 1)

            def other_key_norms(b):
                dve.wait_ge(padded, 3 * (b + 1))
                key_norms(b, UNIT, TP)

            def matrix_parts():
                r32 = NH * RANK
                v.tensor_tensor(
                    UB[:], we("u_t")[0:r32, :].rearrange("p (h d) -> p h d", h=1).to_broadcast([r32, NH, HD]),
                    co("head_r")[0:r32, :].rearrange("p (h d) -> p h d", d=1).to_broadcast([r32, NH, HD]),
                    ALU.mult).then_inc(ub_ready, 1)
                dve.wait_ge(spectrum_product, 1)
                v.tensor_copy(R1T[:], bank[4][:, 0:D])
                v.tensor_copy(R2T[:], bank[4][:, D:2 * D]).then_inc(spectrum_ready, 1)
                dve.wait_ge(gate_abs_ready, 1)
                v.tensor_scalar(gate_sign[:], bank[3][:, :].rearrange("p (j b d) -> p j b d", j=2, b=B), 0.0, 2.0,
                                ALU.is_ge, ALU.mult)
                then(v.tensor_scalar(gate_abs[:], gate_abs[:], 0.25, None, ALU.max))
                then(v.scalar_tensor_tensor(gates[:], gate_sign[:], -1.0, gate_abs[:], ALU.add, ALU.mult))

            dve.wait_ge(silu_exp_ready, 1)
            then(v.tensor_scalar(silu_c[:, 1], silu_c[:, 0], 1.0, None, ALU.add))
            then(v.reciprocal(silu_c[:, 2], silu_c[:, 1]))
            then(v.tensor_tensor(silu_c[:, 3], silu_c[:, 2], we("c_t"), ALU.mult))
            for b in range(B):
                last = v.tensor_copy(silu_rows[:, b], silu_c[:, 3, b:b + 1].to_broadcast([P, P]))
            last.then_inc(silu_ready, 1)
            moments1(0)
            for w in range(B * UNITS):
                if w + 1 < B * UNITS:
                    moments1(w + 1)
                if w == B * UNITS - 1:
                    matrix_parts()
                    metric(0)
                normed1(w)
                if w == 0:
                    dve.wait_ge(mod_product, 1)
                    pm = bank[2][:, 0:6 * B].rearrange("p (j b) -> p j b", b=B)
                    for j, add in ((0, 0.0), (1, 1.0), (3, 0.0), (4, 1.0)):
                        last = v.tensor_scalar(mod[:, j], pm[:, j], add, None, ALU.add)
                    last.then_inc(mod_ready, 1)
                if w == 1:
                    dve.wait_ge(consts_loaded[0], 16)
                    dve.wait_ge(consts_loaded[1], 16)
                    dve.wait_ge(weights_loaded[1], 16)
                    v.tensor_copy(ident_b[:], ident)
                    v.tensor_copy(window_b[:], co("window"))
                    v.scalar_tensor_tensor(bb[:, 1:2], we("b2"), 0.1, we("base"), ALU.mult,
                                           ALU.add).then_inc(consts_b_ready, 1)
                if w == UNITS + 1:
                    signal(0)
            other_key_norms(0)

            def fold():
                for b in range(B):
                    v.tensor_tensor(DEC[:, b], we("decoder"), gates[:, 0, b], ALU.mult)
                    v.tensor_tensor(FB[:, b], we("bias"), gates[:, 1, b], ALU.mult)
                dve.wait_ge(ff_product, 2)
                for b in range(B):
                    v.tensor_tensor(FF[:, b], bank[5][:, 0:D], gates[:, 1, b], ALU.mult)
                dve.wait_ge(heb_product, 1)
                v.tensor_tensor(HEB[:], bank[5][:, D:D + HD].rearrange("p (h d) -> p h d", h=1).to_broadcast([P, NH, HD]),
                                co("head").rearrange("p (h d) -> p h d", d=1).to_broadcast([P, NH, HD]),
                                ALU.mult).then_inc(setup_done, 1)

            def group_ready(n):
                if known(n, 2 * PAIRS):
                    need(dve, scores_copied, n + 1)

            def take8(r, u, between=None):
                src = R if r else S
                found = top8 if r else first8[:, u]
                before = u * GB * ROUNDS
                for k in range(GB):
                    if r:
                        dve.wait_ge(marked, before + GB * (r - 1) + k + 1)
                    v.max(found[:, k], src[:, u, k]).then_inc(top8_found, 1)
                if between is not None:
                    moments_out(between)
                for k in range(GB):
                    dve.wait_ge(top8_found, before + GB * r + k + 1)
                    v.match_replace(R[:, u, k], found[:, k], src[:, u, k], TAKEN).then_inc(marked, 1)
                if r == 0:
                    dve.sem_inc(first8_ready)

            def end_group(n, u):
                if known(n, 2 * PAIRS):
                    dve.wait_ge(marked, (u + 1) * GB * ROUNDS)
                    if u:
                        dve.sem_clear(marked)
                        dve.sem_clear(top8_found)
                    dve.sem_inc(group_taken)

            def normalise(k):
                if known(k, PAIRS):
                    need(dve, rden_ready, k + 1)
                    need(dve, context_ready, 2 * k + 2)
                    v.tensor_tensor(CN[:], pC, RD[:], ALU.mult).then_inc(cn_ready, 1)

            def gate(k):
                if known(k, PAIRS):
                    need(dve, invq_ready, k + 1)
                    need(dve, heb_ready, k)
                    v.scalar_tensor_tensor(G0[:], pN, 0.04, IQ[:], ALU.is_gt, ALU.mult).then_inc(gate_ready, 1)

            def moments(k):
                if known(k, PAIRS):
                    need(dve, x1_copied, k + 1)
                    v.bn_stats(stats2[:], X1[:]).then_inc(stats2_found, 1)

            def moments_out(k):
                if known(k, PAIRS):
                    dve.wait_ge(stats2_found, 1)
                    v.bn_aggr(mv2[:], stats2[:]).then_inc(mv2_ready, 1)
                    dve.sem_clear(stats2_found)

            def body(i):
                n = 2 * i
                more = known(i, PAIRS)
                group_ready(n)
                moments(i - 2)
                end_group(n - 1, 1)
                if more:
                    take8(0, 0, i - 2)
                else:
                    moments_out(i - 2)
                if more:
                    take8(1, 0)
                if isinstance(i, int) and i == 1:
                    metric(1)
                    other_key_norms(1)
                if more:
                    take8(2, 0)
                if isinstance(i, int) and i == 0:
                    fold()
                if more:
                    take8(3, 0)
                if isinstance(i, int) and i == 0:
                    signal(1)
                group_ready(n + 1)
                normalise(i - 1)
                end_group(n, 0)
                if more:
                    take8(0, 1)
                    take8(1, 1)
                if not (isinstance(i, int) and i == 0):
                    gate(i)
                if more:
                    take8(2, 1)
                    take8(3, 1)
                if isinstance(i, int) and i == 0:
                    gate(0)

            run(dve, body)

        @block.tensor
        def _(pe):
            t = nc.tensor
            pe.wait_ge(weights_loaded[0], 16)
            pe.wait_ge(silu_ready, 1)
            for j in range(6):
                last = t.matmul(bank[2][:, j * B:(j + 1) * B], we("wmod")[:, j * D:(j + 1) * D], silu_c[:, 3],
                                start=True, stop=True)
            last.then_inc(mod_product, 1)

            def gate_rows():
                for n, j in enumerate((2, 5)):
                    for b in range(B):
                        at = (n * B + b) * D
                        last = t.matmul(bank[3][:, at:at + D], silu_rows[:, b], we("wmod")[:, j * D:(j + 1) * D],
                                        start=True, stop=True)
                last.then_inc(gate_product, 1)

            def spectrum():
                pe.wait_ge(consts_loaded[1], 16)
                pe.wait_ge(weights_loaded[1], 16)
                for n, (w0, m0, w1, m1) in enumerate((("w_re", "cos", "w_im", "sin"), ("w_im", "cos", "w_re", "msin"))):
                    o = bank[4][:, n * D:(n + 1) * D]
                    t.matmul(o, we(w0), co(m0), start=True, stop=False)
                    last = t.matmul(o, we(w1), co(m1), start=False, stop=True)
                last.then_inc(spectrum_product, 1)

            def turned(w):
                pe.wait_ge(xn1_ready, w + 1)
                need(pe, h_ready, w - 1)
                for c in range(UT):
                    last = t.transpose(bank[w % 2][:, c * P:(c + 1) * P], XN1[:, w % 2, c * P:(c + 1) * P], ident)
                last.then_inc(xt1_ready, 1)

            def hidden(b):
                pe.wait_ge(signal_ready, b + 1)
                t.matmul(bank[2][0:MLP, 16:17], we("w1"), sig[:, 2, b:b + 1], start=True,
                         stop=True).then_inc(hidden_product, 1)

            def metric(b):
                pe.wait_ge(hidden_ready, b + 1)
                t.matmul(bank[2][:, 18:19], we("w2")[0:MLP, :], mlp[:, b:b + 1], start=True,
                         stop=True).then_inc(metric_product, 1)

            def matrices():
                pe.wait_ge(ub_ready, 1)
                r32 = NH * RANK
                t.matmul(bank[5][:, D:D + HD], UB[:].rearrange("p h d -> p (h d)"), we("v")[0:r32, :],
                         start=True, stop=True).then_inc(heb_product, 1)
                pe.wait_ge(spectrum_ready, 1)
                t.matmul(bank[5][:, 0:D], R1T[:], co("cos_n"), start=True, stop=False).then_inc(ff_product, 1)
                t.matmul(bank[5][:, 0:D], R2T[:], co("msin_n"), start=False, stop=True).then_inc(ff_product, 1)

            def scores(i, u):
                n = 2 * i + u
                if known(n, 2 * PAIRS):
                    need(pe, expanded, n + 1)
                    need(pe, scores_copied, n - 1)
                    own = QM2[:, bass.ds(column(i, u), P)]
                    spans = bass.AP(tensor=own.tensor, offset=own.offset,
                                    ap=[list(own.ap[0]), [BLK, GB], [1, SPAN]])
                    t.matmul(pS[u], co("minus_head"), spans, start=True, stop=False)
                    t.matmul(pS[u], ident_b[:], window_b[:].rearrange("p (k j) -> p k j", k=1).to_broadcast([P, GB, SPAN]),
                             start=False, stop=False)
                    for k in range(GB):
                        keys = bass.ds(column(i, u) + k * BLK, SPAN)
                        last = t.matmul(pS[u][:, k], A[:, u, k].rearrange("p h t -> p (h t)"), Q[:, keys],
                                        start=False, stop=(k == GB - 1))
                    last.then_inc(scores_ready, 1)

            pe.wait_ge(consts_loaded[0], 16)
            turned(0)
            for w in range(B * UNITS):
                if w + 1 == B * UNITS - 1:
                    pe.wait_ge(h_ready, w + 1)
                    pe.wait_ge(key_norms_ready, 1)
                    scores(0, 0)
                if w + 1 < B * UNITS:
                    turned(w + 1)
                pe.wait_ge(h_ready, w + 1)
                need(pe, q_ready, w - 1)
                t.matmul(bank[6 + w % 2][:, :], we("enc_q"), HT[:, unit_cols(w)],
                         start=True, stop=True).then_inc(qmm_ready, 1)
                if w == 1:
                    gate_rows()
                if w == 2:
                    spectrum()
                if w == UNITS:
                    hidden(0)
                    metric(0)

            def values(i, u):
                n = 2 * i + u
                if known(n, 2 * PAIRS):
                    need(pe, v_copied, n)
                    if u == 0:
                        need(pe, out_ready, i - 1)
                    need(pe, frame_copied, n + 1)
                    t.matmul(pV, HV[:, u], we("enc_v"), start=True,
                             stop=True).then_inc(v_ready, 1)

            def weights_t(n, u):
                if known(n, 2 * PAIRS):
                    need(pe, weights_ready, n + 1)
                    need(pe, wt_copied, n - 1)
                    for k in range(GB):
                        last = t.transpose(pW[u][:, k], W[:, u, k], ident)
                    last.then_inc(wt_ready, 1)

            def context(i, u):
                n = 2 * i + u
                if known(n, 2 * PAIRS):
                    need(pe, wt_copied, n + 1)
                    need(pe, gate_ready, i + 1)
                    ones = co("parity").rearrange("p (s c) -> p s c", s=2)
                    for a in range(4):
                        for s in range(2):
                            last = t.matmul(pD[a * PQ:(a + 1) * PQ, u * GQ:(u + 1) * GQ], ones[:, s, :],
                                            WT[:, u, :, 2 * a + s, :], start=(s == 0), stop=(s == 1))
                    last.then_inc(den_summed, 1)
                    need(pe, v_copied, n + 1)
                    need(pe, cn_ready, i)
                    for a in range(4):
                        for s in range(2):
                            last = t.matmul(pC[a * PQ:(a + 1) * PQ, u * GQ:(u + 1) * GQ], V[:, u, s, a * PQ:(a + 1) * PQ],
                                            WT[:, u, :, 2 * a + s, :], start=(s == 0), stop=(s == 1))
                    last.then_inc(context_ready, 1)

            def norms(k):
                if known(k, PAIRS):
                    need(pe, den_ready, k)
                    need(pe, heb_ready, k)
                    cols = bass.ds(column(k), P)
                    t.matmul(pN, co("same_head"), Q2[:, cols], start=True, stop=True)
                    t.matmul(pH, HEB[:].rearrange("p h d -> p (h d)"), Q[:, cols], start=True,
                             stop=True).then_inc(norms_ready, 1)

            def attention(k):
                if known(k, PAIRS):
                    need(pe, x1_copied, k)
                    need(pe, h2_ready, k - 1)
                    t.matmul(pA, ident, X[:, bass.ds(k, 1), :].rearrange("p o d -> p (o d)"), start=True, stop=False)
                    need(pe, o_ready, k + 1)
                    t.matmul(pA, O[:], DEC[:, bass.ds(k // PB, 1)].rearrange("p o d -> p (o d)"), start=False,
                             stop=True).then_inc(att_ready, 1)

            def normed_t(k):
                if known(k, PAIRS):
                    need(pe, xn2_ready, k + 1)
                    t.transpose(pT, XN2[:], ident).then_inc(xt2_ready, 1)

            def feed_forward(k):
                if known(k, PAIRS):
                    b = bass.ds(k // PB, 1)
                    need(pe, x1_copied, k + 1)
                    need(pe, v_copied, min(2 * k + 4, 2 * PAIRS) if isinstance(k, int) else 2 * k + 4)
                    t.matmul(pY, ident, X1[:], start=True, stop=False)
                    t.matmul(pY, co("row0"), FB[:, b].rearrange("p o d -> p (o d)"), start=False, stop=False)
                    need(pe, h2_ready, k + 1)
                    t.matmul(pY, H2[:], FF[:, b].rearrange("p o d -> p (o d)"), start=False,
                             stop=True).then_inc(y_ready, 1)

            def body(i):
                values(i - 1, 1)
                if isinstance(i, int) and i == 1:
                    pe.wait_ge(key_norms_ready, 2)
                scores(i, 1)
                if isinstance(i, int) and i == 0:
                    hidden(1)
                    metric(1)
                    pe.wait_ge(q_ready, B * UNITS)
                    pe.wait_ge(setup_done, 1)
                weights_t(2 * i - 1, 1)
                normed_t(i - 2)
                context(i - 1, 1)
                feed_forward(i - 2)
                norms(i)
                values(i, 0)
                scores(i + 1, 0)
                weights_t(2 * i, 0)
                attention(i - 1)
                context(i, 0)

            matrices()
            run(pe, body)


def _constants():
    import numpy as np
    c = np.zeros((P, CONST_W), np.float32)

    def put(name, value):
        a, w = CONST_COLS[name]
        value = np.asarray(value)
        c[:value.shape[0], a:a + w] = value

    p = np.arange(P)
    angle = 2 * np.pi * ((p[:, None] * p[None, :]) % D) / D
    put("ident", np.eye(P))
    put("cos", np.cos(angle))
    put("sin", np.sin(angle))
    put("msin", -np.sin(angle))
    put("cos_n", np.cos(angle) / D)
    put("msin_n", -np.sin(angle) / D)
    put("head", p[:, None] // HD == np.arange(NH)[None, :])
    put("same_head", p[:, None] // HD == p[None, :] // HD)
    q = p % BLK
    off = np.arange(SPAN)[None, :] - q[:, None]
    put("window", np.where((off >= 0) & (off < WINDOW), 0.0, OUTSIDE))
    put("parity", np.broadcast_to(np.arange(2 * PQ)[None, :] // PQ == (np.arange(2 * PQ)[None, :] % PQ) // HD, (P, 2 * PQ)))
    put("row0", np.broadcast_to(p[:, None] == 0, (P, P)))
    put("minus_head", -1.0 * (p[:, None] // HD == p[None, :] // BLK))
    put("head_r", np.arange(NH * RANK)[:, None] // RANK == np.arange(NH)[None, :])
    return c


def kernel(**inputs):
    import numpy as np
    import concourse.bacc as bacc
    from concourse.bass_utils import run_bass_kernel_spmd

    given = {k[3:]: np.asarray(a) for k, a in inputs.items()}
    w = np.zeros((P, WEIGHT_W), np.float32)
    for name, a in (
        ("c_t", given["c"].T), ("wmod", given["wmod"]),
        ("enc_q", given["attn_enc_q"].transpose(1, 0, 2).reshape(D, D)),
        ("enc_v", given["attn_enc_v"].transpose(1, 0, 2).reshape(D, D)),
        ("w1", given["attn_metric_w1"]), ("w2", given["attn_metric_w2"]),
        ("b1", given["attn_metric_b1"].reshape(-1, 1)), ("b2", given["attn_metric_b2"].reshape(-1, 1)),
        ("base", given["attn_base_metric"].reshape(-1, 1)),
        ("u_t", given["attn_hebb_U"].transpose(0, 2, 1).reshape(NH * RANK, HD)),
        ("v", given["attn_hebb_V"].reshape(NH * RANK, HD)),
        ("decoder", given["attn_decoder"]), ("w_re", given["ffn_w_freq_real"]),
        ("w_im", given["ffn_w_freq_imag"]), ("bias", given["ffn_bias"].reshape(1, D)),
    ):
        at, width = WEIGHT_COLS[name]
        w[:a.shape[0], at:at + width] = a
    arrays = {"x": np.ascontiguousarray(given["attn_x"][:, ::-1, :]), "weights": w, "consts": _constants()}

    nc = bacc.Bacc("TRN2", target_bir_lowering=False, num_devices=1)
    aps = [nc.dram_tensor(n, a.shape, F32, kind="ExternalInput").ap() for n, a in arrays.items()]
    aps.append(nc.dram_tensor("out", (B * T, D), F32, kind="ExternalOutput").ap())
    build(nc, *aps)
    r = run_bass_kernel_spmd(nc, [arrays], core_ids=[0])
    return np.ascontiguousarray(r.results[0]["out"].reshape(B, T, D)[:, ::-1, :])
```
